# Optimizing a Trainium2 kernel written in Bass

```python
import numpy as np
import jax
import jax.numpy as jnp

def _softmax(x, axis=-1):
    return jax.nn.softmax(x, axis=axis)

def _gelu(x):
    return jax.nn.gelu(x, approximate=True)

def _silu(x):
    return jax.nn.silu(x)

def _sigmoid(x):
    return jax.nn.sigmoid(x)

def _layernorm(x, axis=-1, eps=1e-05):
    m = jnp.mean(x, axis=axis, keepdims=True)
    v = jnp.var(x, axis=axis, keepdims=True)
    return (x - m) / jnp.sqrt(v + eps)

def _scatter_add(tgt, idx, src, axis=0):
    return tgt.at[idx].add(src)

def _segment_sum(src, seg, n):
    return jax.ops.segment_sum(src, seg, n)
kernel_name = 'mk_decoder_postln_d1_seqx_r4_e36d10'

def setup_inputs(seed: int=0):
    np.random.seed(seed)
    _w = jnp.asarray

    def _rec_inputs():
        import jax
        import jax.numpy as jnp
        _rk = jax.random.key(seed)
        x = 7.22e-05 + 1 * jax.random.normal(jax.random.fold_in(_rk, 1), (16, 256, 256), jnp.float32)
        _lenS = 256 - jax.random.randint(jax.random.fold_in(_rk, 7), (16,), 0, max(1, 256 // 4) + 1, jnp.int32)
        _lenS2 = 120 - jax.random.randint(jax.random.fold_in(_rk, 8), (16,), 0, max(1, 120 // 4) + 1, jnp.int32)
        _ctx_768P = jax.random.normal(jax.random.fold_in(_rk, 11), (16, 16, 192), jnp.float32)
        _ctx_768c = jax.random.dirichlet(jax.random.fold_in(_rk, 511), 0.3 * jnp.ones((16,), jnp.float32), (16, 120))
        _ctx_768t = jnp.einsum('bsk,bkd->bsd', _ctx_768c, _ctx_768P)
        _ctx_768t = _ctx_768t * jax.lax.rsqrt(jnp.mean(jnp.square(_ctx_768t)) + 1e-12) * 0.953939
        ctx_768 = 2.09791e-05 + 1.00001 * (_ctx_768t + 0.3 * jax.random.normal(jax.random.fold_in(_rk, 611), (16, 120, 192), jnp.float32))
        return (x, ctx_768)
    x, ctx_768 = _rec_inputs()

    def _L0_attn_setup():
        import jax, jax.numpy as jnp
        import numpy as np
        D_MODEL = 256
        N_HEADS = 16
        HEAD_DIM = D_MODEL // N_HEADS

        def alibi_slopes(n_heads):
            base = 2.0 ** (-8.0 / n_heads)
            return jnp.asarray([base ** i for i in range(1, n_heads + 1)], dtype=jnp.float32)
        key = jax.random.key(seed)
        kx, kq, kk, kv, ko = jax.random.split(key, 5)
        B, T = (2, 512)
        scale = 0.02
        x = jax.random.normal(kx, (B, T, D_MODEL), dtype=jnp.float32)
        Wq = jax.random.normal(kq, (D_MODEL, D_MODEL), dtype=jnp.float32) * scale
        Wk = jax.random.normal(kk, (D_MODEL, D_MODEL), dtype=jnp.float32) * scale
        Wv = jax.random.normal(kv, (D_MODEL, D_MODEL), dtype=jnp.float32) * scale
        Wo = jax.random.normal(ko, (D_MODEL, D_MODEL), dtype=jnp.float32) * scale
        return {'x': x, 'Wq': Wq, 'Wk': Wk, 'Wv': Wv, 'Wo': Wo}
    _L0_attn_all = _L0_attn_setup()
    _L0_attn_in = {k: v for k, v in _L0_attn_all.items() if k in ('Wq', 'Wk', 'Wv', 'Wo')}
    del _L0_attn_all

    def _L0_xattn_setup():
        import jax, jax.numpy as jnp
        import numpy as np
        HEADS = 16
        DIM_HEAD = 64
        key = jax.random.key(seed)
        ks = jax.random.split(key, 7)
        B, Nq, Dq = (4, 512, 256)
        Nk, Dc = (256, 192)
        inner = HEADS * DIM_HEAD
        sq = 1.0 / np.sqrt(Dq)
        sc = 1.0 / np.sqrt(Dc)
        si = 1.0 / np.sqrt(inner)
        return {'x': jax.random.normal(ks[0], (B, Nq, Dq), dtype=jnp.float32), 'context': jax.random.normal(ks[1], (B, Nk, Dc), dtype=jnp.float32), 'Wq': jax.random.normal(ks[2], (Dq, inner), dtype=jnp.float32) * sq, 'Wk': jax.random.normal(ks[3], (Dc, inner), dtype=jnp.float32) * sc, 'Wv': jax.random.normal(ks[4], (Dc, inner), dtype=jnp.float32) * sc, 'Wo': jax.random.normal(ks[5], (inner, Dq), dtype=jnp.float32) * si, 'bo': jax.random.normal(ks[6], (Dq,), dtype=jnp.float32) * 0.01}
    _L0_xattn_all = _L0_xattn_setup()
    _L0_xattn_in = {k: v for k, v in _L0_xattn_all.items() if k in ('Wq', 'Wk', 'Wv', 'Wo', 'bo')}
    del _L0_xattn_all

    def _L0_ffn_setup():
        import jax, jax.numpy as jnp
        import numpy as np
        D_MODEL = 256
        key = jax.random.key(seed)
        k_x, k_w, k_a1, k_a2 = jax.random.split(key, 4)
        x = jax.random.normal(k_x, (4, 512, D_MODEL), dtype=jnp.float32)
        weight = jax.random.normal(k_w, (D_MODEL, D_MODEL), dtype=jnp.float32) * 0.02
        aux_weight1 = jax.random.normal(k_a1, (D_MODEL, D_MODEL), dtype=jnp.float32) * 0.02
        aux_weight2 = jax.random.normal(k_a2, (D_MODEL, D_MODEL), dtype=jnp.float32) * 0.02
        bias = jnp.zeros((D_MODEL,), dtype=jnp.float32)
        return {'x': x, 'weight': weight, 'aux_weight1': aux_weight1, 'aux_weight2': aux_weight2, 'bias': bias}
    _L0_ffn_all = _L0_ffn_setup()
    _L0_ffn_in = {k: v for k, v in _L0_ffn_all.items() if k in ('weight', 'aux_weight1', 'aux_weight2', 'bias')}
    del _L0_ffn_all
    return {'x': x, 'ctx_768': ctx_768, 'L0_attn_Wq': _L0_attn_in['Wq'], 'L0_attn_Wk': _L0_attn_in['Wk'], 'L0_attn_Wv': _L0_attn_in['Wv'], 'L0_attn_Wo': _L0_attn_in['Wo'], 'L0_xattn_Wq': _L0_xattn_in['Wq'], 'L0_xattn_Wk': _L0_xattn_in['Wk'], 'L0_xattn_Wv': _L0_xattn_in['Wv'], 'L0_xattn_Wo': _L0_xattn_in['Wo'], 'L0_xattn_bo': _L0_xattn_in['bo'], 'L0_ffn_weight': _L0_ffn_in['weight'], 'L0_ffn_aux_weight1': _L0_ffn_in['aux_weight1'], 'L0_ffn_aux_weight2': _L0_ffn_in['aux_weight2'], 'L0_ffn_bias': _L0_ffn_in['bias']}

def reference(x, ctx_768, L0_attn_Wq, L0_attn_Wk, L0_attn_Wv, L0_attn_Wo, L0_xattn_Wq, L0_xattn_Wk, L0_xattn_Wv, L0_xattn_Wo, L0_xattn_bo, L0_ffn_weight, L0_ffn_aux_weight1, L0_ffn_aux_weight2, L0_ffn_bias):
    import jax
    import jax.numpy as jnp

    def _L0_attn_ref(x, Wq, Wk, Wv, Wo):
        import jax, jax.numpy as jnp
        import numpy as np
        D_MODEL = 256
        N_HEADS = 16
        HEAD_DIM = D_MODEL // N_HEADS

        def alibi_slopes(n_heads):
            base = 2.0 ** (-8.0 / n_heads)
            return jnp.asarray([base ** i for i in range(1, n_heads + 1)], dtype=jnp.float32)
        B, T, D = x.shape
        H, hd = (N_HEADS, HEAD_DIM)

        def proj(W):
            return (x @ W.T).reshape(B, T, H, hd).transpose(0, 2, 1, 3)
        q, k, v = (proj(Wq), proj(Wk), proj(Wv))
        scale = hd ** (-0.5)
        scores = jnp.einsum('bhqd,bhkd->bhqk', q, k) * scale
        pos = jnp.arange(T, dtype=jnp.float32)
        dist = jnp.abs(pos[:, None] - pos[None, :])
        causal = pos[:, None] >= pos[None, :]
        slopes = alibi_slopes(H)
        bias = -slopes[:, None, None] * jnp.where(causal, dist, 0.0)
        scores = scores + bias[None]
        scores = jnp.where(causal[None, None], scores, -jnp.inf)
        attn = jax.nn.softmax(scores, axis=-1)
        out = jnp.einsum('bhqk,bhkd->bhqd', attn, v)
        out = out.transpose(0, 2, 1, 3).reshape(B, T, D)
        return out @ Wo.T

    def _L0_xattn_ref(x, context, Wq, Wk, Wv, Wo, bo):
        import jax, jax.numpy as jnp
        import numpy as np
        HEADS = 16
        DIM_HEAD = 64
        B, Nq, _ = x.shape
        Nk = context.shape[1]
        h, dh = (HEADS, DIM_HEAD)
        q = (x @ Wq).reshape(B, Nq, h, dh)
        k = (context @ Wk).reshape(B, Nk, h, dh)
        v = (context @ Wv).reshape(B, Nk, h, dh)
        scale = 1.0 / jnp.sqrt(jnp.asarray(dh, dtype=x.dtype))
        scores = jnp.einsum('bqhd,bkhd->bhqk', q, k) * scale
        attn = jax.nn.softmax(scores, axis=-1)
        out = jnp.einsum('bhqk,bkhd->bqhd', attn, v).reshape(B, Nq, h * dh)
        return out @ Wo + bo

    def _L0_ffn_ref(x, weight, aux_weight1, aux_weight2, bias):
        import jax, jax.numpy as jnp
        import numpy as np
        D_MODEL = 256
        h = jnp.einsum('btc,cd->btd', x, weight)
        h = jnp.einsum('btc,cd->btd', h, aux_weight1)
        h = jnp.einsum('btc,cd->btd', h, aux_weight2)
        return jnp.tanh(h + bias)
    x = _layernorm(x + _L0_attn_ref(x, L0_attn_Wq, L0_attn_Wk, L0_attn_Wv, L0_attn_Wo), axis=-1)
    x = _layernorm(x + _L0_xattn_ref(x, ctx_768, L0_xattn_Wq, L0_xattn_Wk, L0_xattn_Wv, L0_xattn_Wo, L0_xattn_bo), axis=-1)
    x = _layernorm(x + _L0_ffn_ref(x, L0_ffn_weight, L0_ffn_aux_weight1, L0_ffn_aux_weight2, L0_ffn_bias), axis=-1)
    return x

_drawn_inputs = setup_inputs


def setup_inputs(seed=0):
    import zlib

    import numpy as np

    out = dict(_drawn_inputs(seed))
    spreads = {'L0_ffn_bias': (0.0, 0.1)}
    factors = {'L0_attn_Wq': 8.0, 'L0_attn_Wk': 8.0, 'L0_xattn_bo': 6.221}
    for name, (base, spread) in spreads.items():
        noise = np.random.default_rng([zlib.crc32(name.encode()), seed]).standard_normal(out[name].shape)
        drawn = base * np.exp(spread * noise) if base else spread * noise
        out[name] = jnp.asarray(drawn.astype(out[name].dtype))
    for name, factor in factors.items():
        out[name] = (out[name] * factor).astype(out[name].dtype)
    return out
```

```python
from contextlib import ExitStack

import concourse.bass as bass
from concourse import mybir

F32 = mybir.dt.float32
F32R = mybir.dt.float32r
BF16 = mybir.dt.bfloat16
ALU = mybir.AluOpType
ACT = mybir.ActivationFunctionType
AX = mybir.AxisListType

P = 128
T = 256
D = 256
NT = T // P
KD = D // P
H = 16
HD = D // H
DX = 64
NK = 120
DC = 192
KC = 2
PC = DC // KC
SLOT = 32
MX = H * DX // P
EPS = 1e-5
R_AUG = 96
R_MAX = R_AUG + 2
R_ALL = R_AUG + 3

ORDER = ("A.qk B.ck A.v B.cv B.x1t B.cq0 B.cq1 A.n0 A.n1 B.n0 A.n2 B.n1 A.n3 B.n2 A.n4 B.n3 A.n5 "
         "B.mt A.mt B.s0 B.s1 A.s0 B.o0 A.s1 B.s2 A.s2 B.o1 B.s3 A.s3 A.o0 B.o2 A.s4 B.o3 A.s5 B.wo "
         "A.o1 B.x2t A.wo B.ff").split()
FILLS = {st: [s[2:] for s in ORDER if s[0] == st] for st in "AB"}
S_BLOCKS = [("old", 0), ("old", 1), ("new", 0), ("old", 2), ("old", 3), ("new", 1)]

STEPS = {
    "pe_a": FILLS["A"],
    "pe_b": FILLS["B"],
    "act_a": "x_hi q_hi k_hi v mt e0 e1 e2 e3 e4 e5".split(),
    "dve_a": "q_lo k_lo m0 m1 m2 m3 m4 m5 den0 rec0 out0 den1 rec1 out1 add stat0 stat1 aggr0 aggr1 norm0 norm1".split(),
    "pool_a": "x_lo veps rstd x1b".split(),
    "act_b": "k v x_hi q0 q1 mt e0 e1 e2 e3 y_hi tanh".split(),
    "dve_b": ("x_lo m0 m1 m2 m3 rec0 out0 rec1 out1 rec2 out2 rec3 out3 add stat0 stat1 aggr0 aggr1 norm0 norm1 "
              "y_lo bias add3 stat30 stat31 aggr30 aggr31 norm30 norm31").split(),
    "pool_b": "kz0 kz1 q0 q1 veps rstd veps3 rstd3".split(),
}


def build_layer(nc, xT, x, cT, wqT, wkT, wvT, woS, xwq, xwk, xwv, xwo, bo, fwT, fa1, fa2, fb,
                ident_in, mask_in, alibi_in, out):
    NB = x.shape[0]
    scr = [[nc.dram_tensor(f"scr_{w}_{p}", [D, T], F32).ap() for p in ("hi", "lo")] for w in ("q", "k")]
    with ExitStack() as ctx:
        def sb(name, shape, dt=F32):
            return ctx.enter_context(nc.sbuf_tensor(name, shape, dt))

        def sem(name):
            return ctx.enter_context(nc.semaphore(name))

        ps = {st: [ctx.enter_context(nc.psum_tensor(f"ps_{st}{i}", [P, 2, 512], F32)) for i in range(2)] for st in "AB"}

        def slot(st, fill):
            return ps[st][FILLS[st].index(fill) % 2]

        def pair(name, shape):
            return [sb(f"{name}_hi", shape, F32R), sb(f"{name}_lo", shape, F32R)]
        w_q, w_k, w_v = (pair(n, [P, KD, D]) for n in ("w_q", "w_k", "w_v"))
        w_o = sb("w_o", [P, H // 4, D])
        w_xq = pair("w_xq", [P, KD, H * DX])
        w_xk = sb("w_xk", [PC, KC, H * DX])
        w_xv = sb("w_xv", [PC, KC, H * DX])
        w_xo = sb("w_xo", [P, MX, D])
        w_f = pair("w_f", [P, KD, D])
        ident = sb("ident", [P, P])
        ident_b = sb("ident_b", [P, P], BF16)
        mask_b = sb("mask_b", [P, 2, 4, P], BF16)
        ident_r = sb("ident_r", [P, P], F32R)
        ones = sb("ones", [P, SLOT])
        bo_b = sb("bo_b", [P, D])
        fb_b = sb("fb_b", [P, D])

        x_T = sb("x_T", [P, KD, T])
        x_hi = sb("x_hi", [P, KD, T], F32R)
        x_lo = sb("x_lo", [P, KD, T], F32R)
        x_n = sb("x_n", [P, NT, D])
        qk_hi = [sb(f"{w}_hi", [P, KD, T], F32R) for w in "qk"]
        qk_lo = [sb(f"{w}_lo", [P, KD, T], F32R) for w in "qk"]
        q_st = sb("q_st", [P, H, T], F32R)
        k_st = sb("k_st", [P, H, T], F32R)
        v_s = sb("v_s", [P, NT, H, SLOT])
        nmax = sb("nmax", [P, NT, H])
        shift = sb("shift", [H, T], F32R)
        p_old = sb("p_old", [P, 2, 4, T])
        p_new = sb("p_new", [P, 8, P])
        den = sb("den", [P, 2, T])
        o_s = sb("o_s", [P, H // 4, T])
        r1 = sb("r1", [P, NT, D])
        st1 = sb("st1", [P, NT, 6])
        mv1 = sb("mv1", [P, NT, 2])
        ve1 = sb("ve1", [P, NT])
        rs1 = sb("rs1", [P, NT])
        x1 = sb("x1", [P, NT, D])
        x1b = sb("x1b", [P, NT, D])
        half = sb("half", [P, NT])
        own_rows = sb("own_rows", [P, 2])
        c_T = sb("c_T", [PC, KC, NK])
        ck = sb("ck", [P, MX, NK])
        ck_z = sb("ck_z", [P, MX, 2, NK], BF16)
        cv = sb("cv", [NK, H * DX])
        x1_hi = sb("x1_hi", [P, KD, T], F32R)
        x1_lo = sb("x1_lo", [P, KD, T], F32R)
        cq = sb("cq", [P, MX, T])
        cq_r = sb("cq_r", [P, MX, T], BF16)
        nmax_x = sb("nmax_x", [P, NT, H])
        shift_x = sb("shift_x", [P, T], F32R)
        p_x = sb("p_x", [NK, 2, 4, T])
        den_x = sb("den_x", [P, T])
        o_x = sb("o_x", [P, 4, 2, T])
        r2 = sb("r2", [P, NT, D])
        st2 = sb("st2", [P, NT, 6])
        mv2 = sb("mv2", [P, NT, 2])
        ve2 = sb("ve2", [P, NT])
        rs2 = sb("rs2", [P, NT])
        x2 = sb("x2", [P, NT, D])
        x2_hi, x2_lo = x1_hi, x1_lo
        h_f = sb("h_f", [P, NT, D])
        y_n = sb("y_n", [P, NT, D])
        stage = [cq[:].rearrange("p m c -> p (m c)"), p_old[:].rearrange("p g j c -> p (g j c)")]
        mask_f = r1

        sems = {name: sem(name) for name in STEPS}
        ld_xT, ld_x, ld_c = sem("ld_xT"), sem("ld_x"), sem("ld_c")
        ld_const = sem("ld_const")
        ld_plain = sem("ld_plain")
        ld_w = [sem("ld_w0"), sem("ld_w1")]
        w_split = sem("w_split")
        w_hi_done = sem("w_hi_done")
        scr_q, scr_k = sem("scr_q"), sem("scr_k")
        st_q, st_k = sem("st_q"), sem("st_k")
        ld_shift = sem("ld_shift")
        stored = sem("stored")
        set_dve, set_pool, set_pe = sem("set_dve"), sem("set_pool"), sem("set_pe")

        def at(name, b, step):
            return b * len(STEPS[name]) + STEPS[name].index(step) + 1

        def wait(eng, name, b, step):
            eng.wait_ge(sems[name], at(name, b, step))

        def wait_all(eng, *waits):
            values = [(q, v if isinstance(v, int) else eng.to_reg(v)) for q, v in waits]
            for q, v in values:
                eng.wait_ge(q, v)

        def wait_apart(eng, *waits):
            values = [(sems[name], at(name, b, step)) for name, b, step in waits]
            values = [(q, v if isinstance(v, int) else eng.to_reg(v)) for q, v in values]
            eng.wait_ge(ld_const, 64)
            for q, v in values:
                eng.wait_ge(q, v)

        WEIGHTS = [(wqT, w_q), (wkT, w_k), (wvT, w_v), (xwq, w_xq)]
        PLAIN = [(woS, w_o), (xwk, w_xk), (xwv, w_xv), (xwo, w_xo)]
        N_SET_DVE = 13
        N_SET_POOL = 3

        block = ctx.enter_context(nc.Block())

        def run_iterations(eng, a, b):
            def merged(steps_a, steps_b, i):
                for s in ORDER:
                    if s[0] == "A":
                        steps_a(s[2:], i + 1, True)
                    else:
                        steps_b(s[2:], i, not isinstance(i, int))
            for s in FILLS["A"]:
                a(s, 0, False)
            merged(a, b, 0)
            with eng.Fori(1, NB - 1) as i:
                merged(a, b, i)
            for s in FILLS["B"]:
                b(s, NB - 1, True)

        @block.sync
        def _(sp):
            def load_x(b, again):
                if again:
                    wait_all(sp, (sems["act_a"], at("act_a", b - 1, "x_hi")), (sems["pool_a"], at("pool_a", b - 1, "x_lo")))
                sp.dma_start(x_T[:], xT[b]).then_inc(ld_xT, 16)

            def load_xn(b, again):
                if again:
                    wait(sp, "dve_a", b - 1, "add")
                sp.dma_start(x_n[:], x[b].rearrange("(t p) d -> p t d", p=P)).then_inc(ld_x, 16)

            def load_c(b, again):
                if again:
                    wait(sp, "pe_b", b - 1, "cv")
                sp.dma_start(c_T[:], cT[b]).then_inc(ld_c, 16)

            def stacks(b, again):
                for w, (name, stored_, loaded, st, order) in enumerate((
                        ("q", scr_q, st_q, q_st, (0, 1, 0)), ("k", scr_k, st_k, k_st, (0, 0, 1)))):
                    wait_all(sp, (sems["act_a"], at("act_a", b, name + "_hi")), *([(loaded, 48 * b)] if again else []))
                    sp.dma_start(scr[w][0].rearrange("(m p) c -> p m c", p=P), qk_hi[w][:].bitcast(F32)).then_inc(stored_, 16)
                    wait(sp, "dve_a", b, name + "_lo")
                    sp.dma_start(scr[w][1].rearrange("(m p) c -> p m c", p=P), qk_lo[w][:].bitcast(F32)).then_inc(stored_, 16)
                    wait_all(sp, (stored_, 32 * b + 32), *([(sems["pe_a"], at("pe_a", b - 1, "s5"))] if again else []))
                    for i, part in enumerate(order):
                        sp.dma_start(st[HD * i:HD * i + HD].bitcast(F32),
                                     scr[w][part].rearrange("(h r) c -> r h c", r=HD)).then_inc(loaded, 16)

            def shift_row(b):
                wait(sp, "act_a", b, "mt")
                row = q_st[R_MAX:R_ALL].bitcast(F32)
                sp.dma_start(row, shift[:].bitcast(F32)).then_inc(ld_shift, 16)

            def store(b):
                wait(sp, "dve_b", b, "norm31")
                sp.dma_start(out[b].rearrange("(t p) d -> p t d", p=P), y_n[:]).then_inc(stored, 16)

            sp.dma_start(ident[:], ident_in).then_inc(ld_const, 16)
            sp.dma_start(mask_f[:, 0, :].rearrange("p (i c) -> p i c", i=2), mask_in).then_inc(ld_const, 16)
            sp.dma_start(bo_b[:], bo.partition_broadcast(P)).then_inc(ld_const, 16)
            sp.dma_start(fb_b[:], fb.partition_broadcast(P)).then_inc(ld_const, 16)
            load_x(0, False)
            load_c(0, False)
            load_xn(0, False)
            for src, dst in PLAIN:
                sp.dma_start(dst[:], src).then_inc(ld_plain, 16)
            for n, (src, dst) in enumerate(WEIGHTS):
                if n >= 2:
                    sp.wait_ge(w_split, 2 * (n - 1))
                rows, cols = src.shape[0], src.shape[1] * src.shape[2]
                sp.dma_start(stage[n % 2][0:rows, 0:cols], src.rearrange("p k n -> p (k n)")).then_inc(ld_w[n % 2], 16)
            n = len(WEIGHTS)
            sp.wait_ge(w_split, 2 * n)
            sp.dma_start(stage[0][:, 0:512], fa1.rearrange("p k n -> p (k n)")).then_inc(ld_w[0], 16)
            sp.dma_start(stage[0][:, 512:1024], fwT.rearrange("p k n -> p (k n)")).then_inc(ld_w[0], 16)
            sp.dma_start(stage[0][:, 1024:1536], fa2.rearrange("p k n -> p (k n)")).then_inc(ld_w[0], 16)
            for c in range(2):
                if c:
                    sp.wait_ge(set_dve, N_SET_DVE - 2)
                sp.dma_start(stage[1][R_AUG:R_ALL, :], alibi_in[:, c]).then_inc(ld_w[1], 16)

            stacks(0, False)
            shift_row(0)
            load_x(1, True)
            load_xn(1, True)
            with sp.Fori(0, NB - 2) as i:
                stacks(i + 1, True)
                load_c(i + 1, True)
                shift_row(i + 1)
                load_x(i + 2, True)
                load_xn(i + 2, True)
                store(i)
            stacks(NB - 1, True)
            load_c(NB - 1, True)
            shift_row(NB - 1)
            store(NB - 2)
            store(NB - 1)
            sp.wait_ge(stored, 16 * NB)

        @block.tensor
        def _(pe):
            def product(dst, lhs, rhs, ks, first=True, last=True):
                n = 0
                for k in ks:
                    for a, c in ((0, 0), (1, 0), (0, 1)):
                        mm = nc.tensor.matmul(dst, lhs(a, k), rhs(c, k), start=(first and n == 0),
                                              stop=(last and n == 3 * len(ks) - 1))
                        n += 1
                return mm

            X = (x_hi, x_lo)
            X1 = (x1_hi, x1_lo)
            X2 = (x2_hi, x2_lo)

            def product_f32(dst, lhs, rhs, ks):
                for k in ks:
                    mm = nc.tensor.matmul(dst, lhs(k), rhs(k), start=(k == 0), stop=(k == len(ks) - 1))
                return mm

            def a(fill, b, again):
                S = slot("A", fill)
                if fill == "qk":
                    wait(pe, "act_a", b, "x_hi")
                    wait(pe, "pool_a", b, "x_lo")
                    if again:
                        wait(pe, "dve_a", b - 1, "out1")
                    for w, wt in enumerate((w_q, w_k)):
                        for m in range(KD):
                            mm = product(S[:, w, m * T:(m + 1) * T], lambda p, k: wt[p][:, k, m * P:(m + 1) * P],
                                         lambda p, k: X[p][:, k, :], range(KD))
                elif fill == "v":
                    if again:
                        wait(pe, "dve_a", b - 1, "add")
                    for t in range(NT):
                        mm = product(S[:, 0, t * D:(t + 1) * D], lambda p, k: X[p][:, k, t * P:(t + 1) * P],
                                     lambda p, k: w_v[p][:, k, :], range(KD))
                elif fill[0] == "n":
                    n = int(fill[1])
                    if n == 0:
                        wait(pe, "act_a", b, "k_hi")
                        wait(pe, "dve_a", b, "k_lo")
                        pe.wait_ge(st_q, 48 * b + 48)
                        pe.wait_ge(st_k, 48 * b + 48)
                    elif n == 1:
                        wait(pe, "act_a", b, "v")
                    else:
                        wait(pe, "dve_a", b, f"m{n - 2}")
                    per = 4 if n < 2 else 2
                    keys = P if n < 2 else T
                    qt = slice(0, P) if n < 2 else slice(P, T)
                    for bank in range(2):
                        for j in range(per):
                            h = (n * 8 if n < 2 else (n - 2) * 4) + bank * per + j
                            nc.tensor.matmul(S[:, bank, j * keys:(j + 1) * keys], q_st[0:R_MAX, h, qt],
                                             k_st[0:R_MAX, h, 0:keys], start=(j == 0), stop=True, skip_group_check=True)
                        diag = S[:, bank, :].rearrange("p (j c) -> p j c", j=per)[:, :, keys - P:keys]
                        mm = nc.tensor.matmul(diag, ident_b[:], mask_b[:, 0, 0:per, :], start=False, stop=True,
                                              skip_group_check=True)
                elif fill == "mt":
                    wait(pe, "dve_a", b, "m5")
                    for t in range(NT):
                        mm = nc.tensor.transpose(S[0:H, 0, t * P:(t + 1) * P], nmax[:, t, :], ident[:])
                elif fill[0] == "s":
                    n = int(fill[1])
                    kind, g = S_BLOCKS[n]
                    if n == 0:
                        pe.wait_ge(ld_shift, 16 * b + 16)
                        wait(pe, "dve_a", b, "m5")
                    elif n == 1:
                        wait(pe, "act_a", b, "mt")
                    elif n == 4:
                        wait(pe, "act_a", b, "e3")
                        wait(pe, "dve_a", b, "out0")
                    else:
                        wait(pe, "act_a", b, f"e{n - 1 if n in (5,) else n - 2}")
                    per = 2 if kind == "old" else 4
                    keys = slice(0, P) if kind == "old" else slice(P, T)
                    qs = slice(0, T) if kind == "old" else slice(P, T)
                    nq = T if kind == "old" else P
                    for bank in range(2):
                        for j in range(per):
                            h = g * 2 * per + bank * per + j
                            nc.tensor.matmul(S[:, bank, j * nq:(j + 1) * nq], k_st[0:R_ALL, h, keys],
                                             q_st[0:R_ALL, h, qs], start=(j == 0), stop=True, skip_group_check=True)
                        diag = S[:, bank, :].rearrange("p (j c) -> p j c", j=per)[:, :, 0:P]
                        mm = nc.tensor.matmul(diag, ident_b[:], mask_b[:, 1, 0:per, :], start=False, stop=True,
                                              skip_group_check=True)
                elif fill[0] == "o":
                    n = int(fill[1])
                    wait(pe, "act_a", b, f"e{3 * n + 2}")
                    for g in range(2):
                        for j in range(4):
                            h = 8 * n + 4 * g + j
                            nc.tensor.matmul(S[SLOT * j:SLOT * j + SLOT, 0, g * T:(g + 1) * T], v_s[:, 0, h, :],
                                             p_old[:, g, j, :], start=True, stop=True, tile_position=(0, SLOT * j))
                        for j in range(4):
                            h = 8 * n + 4 * g + j
                            mm = nc.tensor.matmul(S[SLOT * j:SLOT * j + SLOT, 0, g * T + P:(g + 1) * T], v_s[:, 1, h, :],
                                                  p_new[:, 4 * g + j, :], start=False, stop=True,
                                                  tile_position=(0, SLOT * j), skip_group_check=True)
                elif fill == "wo":
                    wait(pe, "dve_a", b, "out1")
                    for t in range(NT):
                        mm = product_f32(S[:, 0, t * D:(t + 1) * D], lambda k: o_s[:, k, t * P:(t + 1) * P],
                                         lambda k: w_o[:, k, :], range(H // 4))
                mm.then_inc(sems["pe_a"], 1)

            def b_(fill, b, again):
                S = slot("B", fill)
                if fill == "ck":
                    pe.wait_ge(ld_c, 16 * b + 16)
                    if again:
                        wait(pe, "dve_b", b - 1, "bias")
                    for m in range(MX):
                        mm = product_f32(S[:, m // 4, (m % 4) * NK:(m % 4 + 1) * NK],
                                         lambda k: w_xk[:, k, m * P:(m + 1) * P], lambda k: c_T[:, k, :], range(KC))
                elif fill == "cv":
                    if again:
                        wait(pe, "act_b", b - 1, "y_hi")
                        wait(pe, "dve_b", b - 1, "y_lo")
                    for c in range(2):
                        mm = product_f32(S[0:NK, c, :], lambda k: c_T[:, k, :],
                                         lambda k: w_xv[:, k, c * 512:(c + 1) * 512], range(KC))
                elif fill == "x1t":
                    wait(pe, "dve_a", b, "norm1")
                    wait(pe, "act_b", b, "k")
                    for t in range(NT):
                        for k in range(KD):
                            mm = nc.tensor.transpose(S[:, 0, k * T + t * P:k * T + (t + 1) * P],
                                                     x1[:, t, k * P:(k + 1) * P], ident[:])
                elif fill in ("cq0", "cq1"):
                    n = int(fill[2])
                    if n == 0:
                        wait(pe, "act_b", b, "x_hi")
                        wait(pe, "dve_b", b, "x_lo")
                        wait(pe, "act_b", b, "v")
                    for m in range(4):
                        mm = product(S[:, m // 2, (m % 2) * T:(m % 2 + 1) * T],
                                     lambda p, k: w_xq[p][:, k, (4 * n + m) * P:(4 * n + m + 1) * P],
                                     lambda p, k: X1[p][:, k, :], range(KD))
                elif fill[0] == "n":
                    n = int(fill[1])
                    if n < 2:
                        wait(pe, "act_b", b, f"q{n}")
                        wait(pe, "pool_b", b, f"q{n}")
                        wait(pe, "pool_b", b, "kz1")
                    else:
                        wait(pe, "dve_b", b, f"m{n - 2}")
                    t, half_ = n // 2, n % 2
                    for m in range(4):
                        mm = nc.tensor.matmul(S[:, m // 2, (m % 2) * 2 * NK:(m % 2 + 1) * 2 * NK],
                                              cq_r[:, 4 * half_ + m, t * P:(t + 1) * P],
                                              ck_z[:, 4 * half_ + m].rearrange("p j c -> p (j c)"),
                                              start=True, stop=True)
                elif fill == "mt":
                    wait(pe, "dve_b", b, "m3")
                    for t in range(NT):
                        mm = nc.tensor.transpose(S[0:H, 0, t * P:(t + 1) * P], nmax_x[:, t, :], ident[:])
                elif fill[0] == "s":
                    n = int(fill[1])
                    if n == 0:
                        wait(pe, "act_b", b, "mt")
                    elif n == 1:
                        pass
                    elif n == 2:
                        wait(pe, "act_b", b, "e1")
                    elif n == 3:
                        wait(pe, "act_b", b, "e2")
                    for j in range(4):
                        h = 4 * n + j
                        row = slice(DX * (h % 2), DX * (h % 2) + DX)
                        nc.tensor.matmul(S[0:NK, j % 2, (j // 2) * T:(j // 2 + 1) * T], ck[row, h // 2, :],
                                         cq[row, h // 2, :], start=(j < 2), stop=True, skip_group_check=True)
                    for j in range(4):
                        h = 4 * n + j
                        mm = nc.tensor.matmul(S[0:NK, j % 2, (j // 2) * T:(j // 2 + 1) * T],
                                              ident_r[:, h:h + 1].to_broadcast([P, NK]), shift_x[:],
                                              start=False, stop=True, skip_group_check=True)
                elif fill[0] == "o":
                    n = int(fill[1])
                    wait(pe, "act_b", b, f"e{n}")
                    if n:
                        wait(pe, "dve_b", b, f"out{n - 1}")
                    for part in range(3):
                        for j in range(4):
                            h = 4 * n + j
                            if part < 2:
                                wt = cv[:, h * DX + part * SLOT:h * DX + (part + 1) * SLOT]
                                dst = S[SLOT * j:SLOT * j + SLOT, 0, part * T:(part + 1) * T]
                            else:
                                wt = ones[0:NK, :]
                                dst = S[SLOT * j:SLOT * j + SLOT, 1, 0:T]
                            mm = nc.tensor.matmul(dst, wt, p_x[:, n % 2, 2 * (j % 2) + j // 2, :], start=True, stop=True,
                                                  tile_position=(0, SLOT * j))
                elif fill == "wo":
                    wait(pe, "dve_b", b, "out3")
                    for t in range(NT):
                        mm = product_f32(S[:, 0, t * D:(t + 1) * D],
                                         lambda k: o_x[:, k // 2, k % 2, t * P:(t + 1) * P],
                                         lambda k: w_xo[:, k, :], range(MX))
                elif fill == "x2t":
                    wait(pe, "dve_b", b, "norm1")
                    for t in range(NT):
                        for k in range(KD):
                            mm = nc.tensor.transpose(S[:, 0, k * T + t * P:k * T + (t + 1) * P],
                                                     x2[:, t, k * P:(k + 1) * P], ident[:])
                elif fill == "ff":
                    wait(pe, "act_b", b, "y_hi")
                    wait(pe, "dve_b", b, "y_lo")
                    for t in range(NT):
                        mm = product(S[:, 0, t * D:(t + 1) * D], lambda p, k: X2[p][:, k, t * P:(t + 1) * P],
                                     lambda p, k: w_f[p][:, k, :], range(KD))
                mm.then_inc(sems["pe_b"], 1)

            pe.wait_ge(w_split, 2 * len(WEIGHTS))
            pe.wait_ge(set_dve, N_SET_DVE)
            pe.wait_ge(set_pool, N_SET_POOL)
            pe.wait_ge(ld_w[0], 16 * (len(WEIGHTS) // 2 + 3))
            pe.wait_ge(ld_plain, 16 * len(PLAIN))
            F = ps["B"][0]
            raw = stage[0][:, 0:1536].rearrange("p (w k n) -> p w k n", w=3, k=KD)
            for m in range(KD):
                for k in range(KD):
                    mm = nc.tensor.matmul(F[:, 0, m * D:(m + 1) * D], raw[:, 0, k, m * P:(m + 1) * P], raw[:, 1, k, :],
                                          start=(k == 0), stop=(k == KD - 1))
            mm.then_inc(set_pe, 1)
            pe.wait_ge(set_dve, N_SET_DVE + 1)
            for m in range(KD):
                for k in range(KD):
                    mm = nc.tensor.matmul(F[:, 1, m * D:(m + 1) * D], r2[:, k, m * P:(m + 1) * P], raw[:, 2, k, :],
                                          start=(k == 0), stop=(k == KD - 1))
            mm.then_inc(set_pe, 1)
            pe.wait_ge(set_dve, N_SET_DVE + 3)
            run_iterations(pe, a, b_)

        @block.scalar
        def _(act):
            def a(fill, b, again):
                S = slot("A", fill)
                s = sems["act_a"]
                if fill == "qk":
                    act.wait_ge(ld_xT, 16 * b + 16)
                    if again:
                        wait(act, "pe_a", b - 1, "v")
                    nc.scalar.copy(x_hi[:], x_T[:]).then_inc(s, 1)
                    wait(act, "pe_a", b, "qk")
                    if again:
                        act.wait_ge(scr_k, 32 * b)
                        act.wait_ge(scr_q, 32 * b)
                    for w in range(2):
                        nc.scalar.copy(qk_hi[w][:].rearrange("p m c -> p (m c)"), S[:, w, :]).then_inc(s, 1)
                elif fill == "v":
                    wait(act, "pe_a", b, "v")
                    if again:
                        wait(act, "pe_a", b - 1, "o1")
                    nc.scalar.copy(v_s[:, :, :, 0:HD], S[:, 0, :].rearrange("p (t h d) -> p t h d", t=NT, h=H)).then_inc(s, 1)
                elif fill == "mt":
                    wait(act, "pe_a", b, "mt")
                    if again:
                        act.wait_ge(ld_shift, 16 * b)
                    nc.scalar.copy(shift[:], S[0:H, 0, 0:T]).then_inc(s, 1)
                elif fill[0] == "s":
                    n = int(fill[1])
                    kind, g = S_BLOCKS[n]
                    wait(act, "pe_a", b, fill)
                    if n in (3, 4):
                        wait(act, "pe_a", b, "o0")
                    elif n == 0 and again:
                        wait(act, "pe_a", b - 1, "o1")
                    if kind == "old":
                        dst = p_old[:, g % 2].rearrange("p j c -> p (j c)")
                    else:
                        dst = p_new[:].rearrange("p j c -> p (j c)")
                    nc.scalar.activation(dst, S[:].rearrange("p k c -> p (k c)"), ACT.Exp, scale=HD ** -0.5).then_inc(s, 1)

            def b_(fill, b, again):
                S = slot("B", fill)
                s = sems["act_b"]
                if fill == "ck":
                    wait(act, "pe_b", b, "ck")
                    if again:
                        wait(act, "pe_b", b - 1, "s3")
                    nc.scalar.copy(ck[:].rearrange("p (k m) c -> p k (m c)", k=2), S[:, :, 0:4 * NK]).then_inc(s, 1)
                elif fill == "cv":
                    wait(act, "pe_b", b, "cv")
                    if again:
                        wait(act, "pe_b", b - 1, "o3")
                    nc.scalar.copy(cv[:].rearrange("p (k c) -> p k c", k=2), S[0:NK, :, :]).then_inc(s, 1)
                elif fill == "x1t":
                    wait(act, "pe_b", b, "x1t")
                    if again:
                        wait(act, "pe_b", b - 1, "ff")
                    nc.scalar.copy(x1_hi[:].rearrange("p k c -> p (k c)"), S[:, 0, :]).then_inc(s, 1)
                elif fill in ("cq0", "cq1"):
                    n = int(fill[2])
                    wait(act, "pe_b", b, fill)
                    if again:
                        wait(act, "pe_b", b - 1, "s3")
                    nc.scalar.copy(cq[:, 4 * n:4 * n + 4].rearrange("p (k m) c -> p k (m c)", k=2), S[:]).then_inc(s, 1)
                elif fill == "mt":
                    wait(act, "pe_b", b, "mt")
                    nc.scalar.copy(shift_x[0:H, :], S[0:H, 0, 0:T]).then_inc(s, 1)
                elif fill[0] == "s":
                    n = int(fill[1])
                    wait(act, "pe_b", b, fill)
                    if n >= 2:
                        wait(act, "pe_b", b, f"o{n - 2}")
                    nc.scalar.activation(p_x[:, n % 2].rearrange("p j c -> p (j c)"),
                                         S[0:NK].rearrange("p k c -> p (k c)"), ACT.Exp, scale=DX ** -0.5).then_inc(s, 1)
                elif fill == "x2t":
                    wait(act, "pe_b", b, "x2t")
                    nc.scalar.copy(x2_hi[:].rearrange("p k c -> p (k c)"), S[:, 0, :]).then_inc(s, 1)
                elif fill == "ff":
                    wait(act, "dve_b", b, "bias")
                    nc.scalar.activation(h_f[:], h_f[:], ACT.Tanh).then_inc(s, 1)

            nc.scalar.preload_act_table(ACT.Exp)
            for n, (src, dst) in enumerate(WEIGHTS):
                rows, cols = src.shape[0], src.shape[1] * src.shape[2]
                act.wait_ge(ld_w[n % 2], 16 * (n // 2 + 1))
                nc.scalar.copy(dst[0][:].rearrange("p k n -> p (k n)"), stage[n % 2][0:rows, 0:cols])\
                    .then_inc(w_hi_done, 1)
            run_iterations(act, a, b_)

        @block.vector
        def _(dve):
            def layer_stats(res, S, skip, stats, mv, name, b, add, stat, aggr):
                s = sems[name]
                nc.vector.tensor_tensor(res[:].rearrange("p t d -> p (t d)"), S, skip[:].rearrange("p t d -> p (t d)"),
                                        ALU.add).then_inc(s, 1)
                wait(dve, name, b, add)
                for t in range(NT):
                    nc.vector.bn_stats(stats[:, t, :], res[:, t, :]).then_inc(s, 1)
                for t in range(NT):
                    wait_apart(dve, (name, b, f"{stat}{t}"))
                    nc.vector.bn_aggr(mv[:, t, :], stats[:, t, :]).then_inc(s, 1)

            def normalise(dst, res, mv, rstd, name):
                for t in range(NT):
                    nc.vector.tensor_scalar(dst[:, t, :], res[:, t, :], mv[:, t, 0:1], rstd[:, t:t + 1], ALU.subtract,
                                            ALU.mult).then_inc(sems[name], 1)

            def a(fill, b, again):
                S = slot("A", fill)
                s = sems["dve_a"]
                if fill == "qk":
                    for w, name in enumerate(("q_hi", "k_hi")):
                        wait(dve, "act_a", b, name)
                        if again:
                            dve.wait_ge((scr_q, scr_k)[w], 32 * b)
                        nc.vector.tensor_tensor(qk_lo[w][:].rearrange("p m c -> p (m c)"), S[:, w, :],
                                                qk_hi[w][:].bitcast(F32).rearrange("p m c -> p (m c)"),
                                                ALU.subtract).then_inc(s, 1)
                elif fill[0] == "n":
                    n = int(fill[1])
                    wait(dve, "pe_a", b, fill)
                    if n == 0 and again:
                        wait(dve, "pe_a", b - 1, "mt")
                    if n < 2:
                        src = S[:].rearrange("p k (j c) -> p (k j) c", c=P)
                        dst = nmax[:, 0, 8 * n:8 * n + 8]
                    else:
                        src = S[:].rearrange("p k (j c) -> p (k j) c", c=T)
                        dst = nmax[:, 1, 4 * (n - 2):4 * (n - 2) + 4]
                    nc.vector.tensor_reduce(dst, src, AX.X, ALU.max, negate=True).then_inc(s, 1)
                elif fill[0] == "o":
                    n = int(fill[1])
                    wait_apart(dve, ("pe_a", b, fill))
                    flat = den[:].rearrange("p g c -> p (g c)")
                    nc.vector.stream_shuffle(flat, S[:, 0, :], [HD] * SLOT).then_inc(s, 1)
                    wait(dve, "dve_a", b, f"den{n}")
                    nc.vector.reciprocal(flat, flat).then_inc(s, 1)
                    wait(dve, "dve_a", b, f"rec{n}")
                    if again and n == 0:
                        wait(dve, "pe_a", b - 1, "wo")
                    nc.vector.tensor_tensor(o_s[:, 2 * n:2 * n + 2].rearrange("p g c -> p (g c)"), S[:, 0, :], flat,
                                            ALU.mult).then_inc(s, 1)
                elif fill == "wo":
                    wait(dve, "pe_a", b, "wo")
                    dve.wait_ge(ld_x, 16 * b + 16)
                    layer_stats(r1, S[:, 0, :], x_n, st1, mv1, "dve_a", b, "add", "stat", "aggr")
                    wait(dve, "pool_a", b, "rstd")
                    if again:
                        wait(dve, "pe_b", b - 1, "x1t")
                        wait(dve, "pool_a", b - 1, "x1b")
                    normalise(x1, r1, mv1, rs1, "dve_a")

            def b_(fill, b, again):
                S = slot("B", fill)
                s = sems["dve_b"]
                if fill == "x1t":
                    wait(dve, "act_b", b, "x_hi")
                    nc.vector.tensor_tensor(x1_lo[:].rearrange("p k c -> p (k c)"), S[:, 0, :],
                                            x1_hi[:].bitcast(F32).rearrange("p k c -> p (k c)"),
                                            ALU.subtract).then_inc(s, 1)
                elif fill[0] == "n":
                    n = int(fill[1])
                    wait(dve, "pe_b", b, fill)
                    if again and n == 0:
                        wait(dve, "pe_b", b - 1, "mt")
                    t, half_ = n // 2, n % 2
                    nc.vector.tensor_reduce(nmax_x[:, t, 8 * half_:8 * half_ + 8].rearrange("p (k j) -> p k j", k=2),
                                            S[:, :, 0:4 * NK].rearrange("p k (j c) -> p k j c", c=NK), AX.X, ALU.max,
                                            negate=True).then_inc(s, 1)
                elif fill[0] == "o":
                    n = int(fill[1])
                    wait(dve, "pe_b", b, fill)
                    nc.vector.reciprocal(den_x[:], S[:, 1, 0:T]).then_inc(s, 1)
                    wait(dve, "dve_b", b, f"rec{n}")
                    if again and n == 0:
                        wait(dve, "pe_b", b - 1, "wo")
                    nc.vector.tensor_tensor(o_x[:, n], S[:, 0, :].rearrange("p (k c) -> p k c", k=2),
                                            den_x[:].rearrange("p (o c) -> p o c", o=1).to_broadcast([P, 2, T]),
                                            ALU.mult).then_inc(s, 1)
                elif fill == "wo":
                    wait(dve, "pe_b", b, "wo")
                    wait(dve, "pool_a", b, "x1b")
                    layer_stats(r2, S[:, 0, :], x1b, st2, mv2, "dve_b", b, "add", "stat", "aggr")
                    wait(dve, "pool_b", b, "rstd")
                    if again:
                        wait(dve, "pe_b", b - 1, "x2t")
                    normalise(x2, r2, mv2, rs2, "dve_b")
                elif fill == "x2t":
                    wait(dve, "act_b", b, "y_hi")
                    nc.vector.tensor_tensor(x2_lo[:].rearrange("p k c -> p (k c)"), S[:, 0, :],
                                            x2_hi[:].bitcast(F32).rearrange("p k c -> p (k c)"),
                                            ALU.subtract).then_inc(s, 1)
                elif fill == "ff":
                    wait(dve, "pe_b", b, "ff")
                    nc.vector.tensor_tensor(h_f[:], S[:, 0, :].rearrange("p (t d) -> p t d", t=NT),
                                            fb_b[:].rearrange("p (o d) -> p o d", o=1).to_broadcast([P, NT, D]),
                                            ALU.add).then_inc(s, 1)
                    wait(dve, "act_b", b, "tanh")
                    layer_stats(r2, h_f[:].rearrange("p t d -> p (t d)"), x2, st2, mv2, "dve_b", b, "add3", "stat3", "aggr3")
                    wait(dve, "pool_b", b, "rstd3")
                    if again:
                        dve.wait_ge(stored, 16 * b)
                    normalise(y_n, r2, mv2, rs2, "dve_b")

            n_set = [0]

            def setup(ins):
                n_set[0] += 1
                ins.then_inc(set_dve, 1)
            dve.wait_ge(ld_const, 64)
            setup(nc.vector.tensor_copy(ident_b[:], ident[:]))
            for i in range(2):
                setup(nc.vector.tensor_copy(mask_b[:, i], mask_f[:, 0, i * P:(i + 1) * P].rearrange("p (o c) -> p o c", o=1).to_broadcast([P, 4, P])))
            setup(nc.vector.tensor_copy(ident_r[:], ident[:]))
            setup(nc.vector.memset(half[:], -0.5))
            setup(nc.vector.memset(ones[:], 1.0))
            setup(nc.vector.memset(v_s[:, :, :, HD:SLOT], 1.0))
            setup(nc.vector.memset(q_st[:].bitcast(F32), 0.0))
            setup(nc.vector.memset(k_st[:].bitcast(F32), 0.0))
            dve.wait_ge(set_dve, 9)
            setup(nc.vector.memset(q_st[R_AUG:R_ALL].bitcast(F32), 1.0))
            for n, (src, dst) in enumerate(WEIGHTS):
                rows, cols = src.shape[0], src.shape[1] * src.shape[2]
                dve.wait_ge(w_hi_done, n + 1)
                nc.vector.tensor_tensor(dst[1][:].rearrange("p k n -> p (k n)"), stage[n % 2][0:rows, 0:cols],
                                        dst[0][:].bitcast(F32).rearrange("p k n -> p (k n)"), ALU.subtract)\
                    .then_inc(w_split, 2)
            for c in range(2):
                dve.wait_ge(ld_w[1], 16 * (len(WEIGHTS) // 2 + 1 + c))
                setup(nc.vector.tensor_copy(k_st[R_AUG:R_ALL, 8 * c:8 * c + 8].rearrange("p h c -> p (h c)"),
                                            stage[1][R_AUG:R_ALL, :]))
            setup(nc.vector.memset(shift_x[:].bitcast(F32), 0.0))
            assert n_set[0] == N_SET_DVE
            dve.wait_ge(set_pe, 1)
            setup(nc.vector.tensor_copy(r2[:].rearrange("p k c -> p (k c)"), ps["B"][0][:, 0, :]))
            dve.wait_ge(set_pe, 2)
            setup(nc.vector.tensor_copy(w_f[0][:].rearrange("p k c -> p (k c)"), ps["B"][0][:, 1, :]))
            dve.wait_ge(set_dve, N_SET_DVE + 2)
            setup(nc.vector.tensor_tensor(w_f[1][:].rearrange("p k c -> p (k c)"), ps["B"][0][:, 1, :],
                                          w_f[0][:].bitcast(F32).rearrange("p k c -> p (k c)"), ALU.subtract))
            run_iterations(dve, a, b_)

        @block.gpsimd
        def _(pool):
            def rstd(mv, ve, rs, name, b, eps_step, aggr):
                s = sems[name]
                nc.gpsimd.tensor_scalar(ve[:], mv[:, :, 1], EPS, None, ALU.add).then_inc(s, 1)
                wait(pool, name, b, eps_step)
                nc.gpsimd.tensor_tensor(rs[:], ve[:], half[:], ALU.pow).then_inc(s, 1)

            def a(fill, b, again):
                s = sems["pool_a"]
                if fill == "qk":
                    wait(pool, "act_a", b, "x_hi")
                    if again:
                        wait(pool, "pe_a", b - 1, "v")
                    nc.gpsimd.tensor_tensor(x_lo[:], x_T[:], x_hi[:].bitcast(F32), ALU.subtract).then_inc(s, 1)
                elif fill == "wo":
                    wait_apart(pool, ("dve_a", b, "aggr1"))
                    rstd(mv1, ve1, rs1, "pool_a", b, "veps", "aggr1")
                    wait(pool, "dve_a", b, "norm1")
                    if again:
                        wait(pool, "dve_b", b - 1, "add")
                    nc.gpsimd.tensor_tensor(x1b[:], x1[:], bo_b[:].rearrange("p (o d) -> p o d", o=1).to_broadcast([P, NT, D]),
                                            ALU.add).then_inc(s, 1)

            def b_(fill, b, again):
                s = sems["pool_b"]
                if fill == "ck":
                    wait_apart(pool, ("act_b", b, "k"), *([("pe_b", b - 1, "n3")] if again else []))
                    for j in range(2):
                        nc.gpsimd.tensor_scalar(ck_z[:, :, j, :], ck[:], own_rows[:, j:j + 1], 1.0, ALU.mult,
                                                ALU.mult).then_inc(s, 1)
                elif fill in ("cq0", "cq1"):
                    n = int(fill[2])
                    wait_apart(pool, ("act_b", b, f"q{n}"), *([("pe_b", b - 1, "n3")] if again else []))
                    nc.gpsimd.tensor_copy(cq_r[:, 4 * n:4 * n + 4], cq[:, 4 * n:4 * n + 4]).then_inc(s, 1)
                elif fill == "wo":
                    wait_apart(pool, ("dve_b", b, "aggr1"))
                    rstd(mv2, ve2, rs2, "pool_b", b, "veps", "aggr1")
                elif fill == "ff":
                    wait_apart(pool, ("dve_b", b, "aggr31"))
                    rstd(mv2, ve2, rs2, "pool_b", b, "veps3", "aggr31")

            nc.gpsimd.memset(own_rows[:], 0.0).then_inc(set_pool, 1)
            pool.wait_ge(set_pool, 1)
            for j in range(2):
                nc.gpsimd.memset(own_rows[DX * j:DX * j + DX, j:j + 1], 1.0).then_inc(set_pool, 1)
            pool.wait_ge(set_pool, 3)
            pool.wait_ge(set_dve, N_SET_DVE)
            run_iterations(pool, a, b_)


def kernel(x, ctx_768, L0_attn_Wq, L0_attn_Wk, L0_attn_Wv, L0_attn_Wo, L0_xattn_Wq, L0_xattn_Wk, L0_xattn_Wv,
           L0_xattn_Wo, L0_xattn_bo, L0_ffn_weight, L0_ffn_aux_weight1, L0_ffn_aux_weight2, L0_ffn_bias):
    import numpy as np
    import concourse.bacc as bacc
    from concourse.bass_utils import run_bass_kernel_spmd

    def rows(w, p=P):
        w = np.asarray(w)
        return np.ascontiguousarray(w.reshape(-1, p, w.shape[-1]).transpose(1, 0, 2))

    x = np.ascontiguousarray(x)
    nb = x.shape[0]
    wo = np.asarray(L0_attn_Wo).T.reshape(H // 4, 4, HD, D)
    wo_slots = np.zeros((H // 4, 4, SLOT, D), wo.dtype)
    wo_slots[:, :, :HD] = wo
    xwo = np.asarray(L0_xattn_Wo).reshape(4, 4, 2, SLOT, D).transpose(0, 2, 1, 3, 4)
    q, k = np.arange(P)[:, None], np.arange(P)[None, :]
    mask = np.where(np.stack([k <= q, q <= k], 1), 0.0, -1e30).astype(np.float32)
    slopes = np.array([(2.0 ** (-8.0 / H)) ** i for i in range(1, H + 1)], np.float32)
    alibi = (slopes[:, None] * np.arange(T, dtype=np.float32)[None, :]) * np.float32(HD ** 0.5)
    hi = (alibi.view(np.uint32) & np.uint32(0xFFFFF000)).view(np.float32)
    aug = np.stack([hi, alibi - hi, np.ones_like(hi)]).reshape(3, 2, H * T // 2)

    arrays = {
        "xT": x.transpose(0, 2, 1).reshape(nb, KD, P, T).transpose(0, 2, 1, 3),
        "x": x,
        "cT": np.asarray(ctx_768).transpose(0, 2, 1).reshape(nb, KC, PC, NK).transpose(0, 2, 1, 3),
        "wqT": rows(np.asarray(L0_attn_Wq).T), "wkT": rows(np.asarray(L0_attn_Wk).T), "wvT": rows(np.asarray(L0_attn_Wv).T),
        "woS": rows(wo_slots.reshape(-1, D)),
        "xwq": rows(L0_xattn_Wq), "xwk": rows(L0_xattn_Wk, PC), "xwv": rows(L0_xattn_Wv, PC),
        "xwo": rows(xwo.reshape(-1, D)), "bo": np.asarray(L0_xattn_bo),
        "fwT": rows(np.asarray(L0_ffn_weight).T), "fa1": rows(L0_ffn_aux_weight1), "fa2": rows(L0_ffn_aux_weight2),
        "fb": np.asarray(L0_ffn_bias),
        "ident_in": np.eye(P, dtype=np.float32), "mask_in": mask, "alibi_in": aug,
    }
    nc = bacc.Bacc("TRN2", target_bir_lowering=False, num_devices=1)
    feeds, args = {}, []
    for name, a in arrays.items():
        feeds[f"in_{name}"] = np.ascontiguousarray(a)
        args.append(nc.dram_tensor(f"in_{name}", a.shape, mybir.dt.from_np(a.dtype), kind="ExternalInput").ap())
    out = nc.dram_tensor("out", x.shape, F32, kind="ExternalOutput").ap()
    build_layer(nc, *args, out)
    return run_bass_kernel_spmd(nc, [feeds], core_ids=[0]).results[0]["out"]
```

```python
from contextlib import ExitStack

import concourse.bass as bass
from concourse import mybir

F32 = mybir.dt.float32
F32R = mybir.dt.float32r
BF16 = mybir.dt.bfloat16
ALU = mybir.AluOpType
ACT = mybir.ActivationFunctionType
AX = mybir.AxisListType

P = 128
T = 256
D = 256
NT = T // P
KD = D // P
H = 16
HD = D // H
DX = 64
NK = 120
DC = 192
KC = 2
PC = DC // KC
SLOT = 32
MX = H * DX // P
EPS = 1e-5
R_AUG = 96
R_MAX = R_AUG + 2
R_ALL = R_AUG + 3

ORDER = ("C.xn A.n0 B.xn B.ck A.n1 C.x2t A.n2 A.v C.ff B.x1t A.n3 A.n4 C.res B.cq0 A.n5 C.nrm B.cq1 A.mt B.n0 B.cv0 "
         "B.n1 X.x B.n2 B.cv1 B.n3 A.s0 A.s1 B.mt A.s2 B.s0 B.s1 X.qk B.o0 A.s3 B.s2 A.o0 B.o1 B.s3 A.s4 B.o2 A.s5 "
         "B.o3 A.o1 B.wo A.wo").split()
OFFSET = {"X": 2, "A": 1, "B": 0, "C": -1}
NO_FILL = ("xn", "res", "nrm", "x")
AX_FILLS = [s for s in ORDER if s[0] in "AX" and s[2:] not in NO_FILL]
BC_FILLS = [s for s in ORDER if s[0] in "BC" and s[2:] not in NO_FILL]
S_BLOCKS = [("old", 0), ("old", 1), ("new", 0), ("old", 2), ("old", 3), ("new", 1)]

STEPS = {
    "pe_x": ["qk"],
    "pe_a": [s[2:] for s in AX_FILLS if s[0] == "A"],
    "pe_b": [s[2:] for s in BC_FILLS if s[0] == "B"],
    "pe_c": [s[2:] for s in BC_FILLS if s[0] == "C"],
    "act_x": "x_hi q_hi k_hi".split(),
    "dve_x": "q_lo k_lo".split(),
    "pool_x": ["x_lo"],
    "act_a": "v mt e0 e1 e2 e3 e4 e5".split(),
    "dve_a": "m0 m1 m2 m3 m4 m5 turn0 rec0 den0 out0 turn1 rec1 den1 out1 add stat0 stat1 aggr0 aggr1".split(),
    "pool_a": "veps rstd".split(),
    "act_b": "k_hi0 k_hi1 x_hi q0 q1 v0 v1 mt e0 e1 e2 e3".split(),
    "dve_b": ("norm0 norm1 k_lo0 k_lo1 x_lo q_lo0 q_lo1 m0 m1 m2 m3 " +
              " ".join(f"turn{n} rec{n} den{n} out{n}" for n in range(4)) + " add stat0 stat1 aggr0 aggr1").split(),
    "pool_b": "x1b veps rstd".split(),
    "act_c": "y_hi tanh".split(),
    "dve_c": "norm0 norm1 y_lo bias add stat0 stat1 aggr0 aggr1 out0 out1".split(),
    "pool_c": "veps rstd".split(),
}


def build_layer(nc, xT, x, cT, wqT, wkT, wvT, woS, xwq, xwk, xwv, xwo, bo, fwT, fa1, fa2, fb,
                ident_in, mask_in, alibi_in, out):
    NB = x.shape[0]
    scr = [[nc.dram_tensor(f"scr_{w}_{p}", [D, T], F32).ap() for p in ("hi", "lo")] for w in ("q", "k")]
    with ExitStack() as ctx:
        def sb(name, shape, dt=F32):
            return ctx.enter_context(nc.sbuf_tensor(name, shape, dt))

        def sem(name):
            return ctx.enter_context(nc.semaphore(name))

        ps = {st: [ctx.enter_context(nc.psum_tensor(f"ps_{st}{i}", [P, 2, 512], F32)) for i in range(2)] for st in "AB"}

        def slot(st, fill):
            if fill in NO_FILL:
                return None
            fills = AX_FILLS if st in "AX" else BC_FILLS
            return ps["A" if st in "AX" else "B"][fills.index(f"{st}.{fill}") % 2]

        def pair(name, shape):
            return [sb(f"{name}_hi", shape, F32R), sb(f"{name}_lo", shape, F32R)]
        w_q, w_k, w_v = (pair(n, [P, KD, D]) for n in ("w_q", "w_k", "w_v"))
        w_o = sb("w_o", [P, H // 4, D])
        w_xq = pair("w_xq", [P, KD, H * DX])
        w_xk = sb("w_xk", [PC, KC, H * DX])
        w_xv = sb("w_xv", [PC, KC, H * DX])
        w_xo = sb("w_xo", [P, MX, D])
        w_f = pair("w_f", [P, KD, D])
        ident_r = sb("ident", [P, P], F32R)
        ident = ident_r[:].bitcast(F32)
        ident_b = sb("ident_b", [P, P], BF16)
        mask_b = sb("mask_b", [P, 2, 4, P], BF16)
        ones = sb("ones", [P, SLOT])
        bo_b = sb("bo_b", [P, D])
        fb_b = sb("fb_b", [P, D])

        x_T = sb("x_T", [P, KD, T])
        x_hi = sb("x_hi", [P, KD, T], F32R)
        x_lo = sb("x_lo", [P, KD, T], F32R)
        x_n = sb("x_n", [P, NT, D])
        qk_hi = [sb(f"{w}_hi", [P, KD, T], F32R) for w in "qk"]
        qk_lo = [sb(f"{w}_lo", [P, KD, T], F32R) for w in "qk"]
        q_st = sb("q_st", [P, H, T], F32R)
        k_st = sb("k_st", [P, H, T], F32R)
        v_s = sb("v_s", [P, NT, H, SLOT])
        nmax = sb("nmax", [P, NT, H])
        shift = sb("shift", [H, T], F32R)
        p_old = sb("p_old", [P, 2, 4, T])
        p_new = sb("p_new", [P, 8, P])
        turned = sb("turned", [P, 2 * T])
        rec = sb("rec", [P, 2 * T // SLOT])
        den = sb("den", [P, 2, T])
        o_s = sb("o_s", [P, H // 4, T])
        r1 = sb("r1", [P, NT, D])
        st1 = sb("st1", [P, NT, 6])
        mv1 = sb("mv1", [P, NT, 2])
        ve1 = sb("ve1", [P, NT])
        rs1 = sb("rs1", [P, NT])
        x1 = sb("x1", [P, NT, D])
        x1b = sb("x1b", [P, NT, D])
        half = sb("half", [P, NT])
        own_rows = sb("own_rows", [P, 2])
        c_T = sb("c_T", [PC, KC, NK])
        ck = pair("ck", [P, MX, 2, NK])
        cv = sb("cv", [NK, H * DX])
        x1_hi = sb("x1_hi", [P, KD, T], F32R)
        x1_lo = sb("x1_lo", [P, KD, T], F32R)
        cq = pair("cq", [P, MX, T])
        nmax_x = sb("nmax_x", [P, NT, H])
        shift_x = sb("shift_x", [P, T], F32R)
        p_x = sb("p_x", [NK, 2, 4, T])
        o_x = sb("o_x", [P, 4, 2, T])
        r2 = sb("r2", [P, NT, D])
        st2 = sb("st2", [P, NT, 6])
        mv2 = sb("mv2", [P, NT, 2])
        ve2 = sb("ve2", [P, NT])
        rs2 = sb("rs2", [P, NT])
        x2 = sb("x2", [P, NT, D])
        x2_hi, x2_lo = x1_hi, x1_lo
        h_f = sb("h_f", [P, NT, D])
        y_n = h_f
        stage = [o_x[:].rearrange("p n k c -> p (n k c)"), p_old[:].rearrange("p g j c -> p (g j c)")]
        mask_f, ident_f = r1[:, 0, :], r1[:, 1, 0:P]
        alibi_stage = [w_xo[:].rearrange("p n c -> p (n c)"), p_x[:].rearrange("p n j c -> p (n j c)")]

        sems = {name: sem(name) for name in STEPS}
        ld_xT, ld_x, ld_c = sem("ld_xT"), sem("ld_x"), sem("ld_c")
        ld_const = sem("ld_const")
        ld_plain = sem("ld_plain")
        ld_w = [sem(f"ld_w{n}") for n in range(4)]
        ld_alibi, ld_bias, ld_ffn = sem("ld_alibi"), sem("ld_bias"), sem("ld_ffn")
        w_split = sem("w_split")
        w_hi_done = sem("w_hi_done")
        scr_q, scr_k = sem("scr_q"), sem("scr_k")
        st_q, st_k = sem("st_q"), sem("st_k")
        ld_shift = sem("ld_shift")
        stored = sem("stored")
        set_dve, set_pool, set_pe = sem("set_dve"), sem("set_pool"), sem("set_pe")

        def at(name, b, step):
            return b * len(STEPS[name]) + STEPS[name].index(step) + 1

        def wait(eng, name, b, step):
            eng.wait_ge(sems[name], at(name, b, step))

        def wait_all(eng, *waits):
            values = [(q, v if isinstance(v, int) else eng.to_reg(v)) for q, v in waits]
            for q, v in values:
                eng.wait_ge(q, v)

        def wait_apart(eng, *waits):
            values = [(sems[name], at(name, b, step)) for name, b, step in waits]
            values = [(q, v if isinstance(v, int) else eng.to_reg(v)) for q, v in values]
            eng.wait_ge(ld_const, 32)
            for q, v in values:
                eng.wait_ge(q, v)

        PLAIN = [(woS, w_o), (xwk, w_xk), (xwv, w_xv), (xwo, w_xo)]
        WEIGHTS = [(wqT, w_q, stage[0][:, 0:512]), (wkT, w_k, stage[0][:, 512:1024]), (wvT, w_v, stage[0][:, 1024:1536]),
                   (xwq, w_xq, stage[1])]
        N_SET = 13
        N_SET_POOL = 4

        block = ctx.enter_context(nc.Block())

        def run_iterations(eng, x, a, b, c, between=lambda: None):
            steps = {"X": x, "A": a, "B": b, "C": c}

            def iteration(i, stages, first=""):
                for s in ORDER:
                    if s[0] in stages:
                        steps[s[0]](s[2:], i + OFFSET[s[0]], s[0] not in first)

            iteration(-2, "X", "X")
            iteration(-1, "XA", "A")
            between()
            iteration(0, "XAB", "B")
            iteration(1, "XABC", "C")
            with eng.Fori(2, NB - 2) as i:
                iteration(i, "XABC")
            iteration(NB - 2, "ABC")
            iteration(NB - 1, "BC")
            iteration(NB, "C")

        @block.sync
        def _(sp):
            def load_x(b, again):
                if again:
                    wait_all(sp, (sems["act_x"], at("act_x", b - 1, "x_hi")), (sems["pool_x"], at("pool_x", b - 1, "x_lo")))
                sp.dma_start(x_T[:], xT[b]).then_inc(ld_xT, 16)

            def load_xn(b, again):
                if again:
                    wait(sp, "dve_a", b - 1, "add")
                sp.dma_start(x_n[:], x[b].rearrange("(t p) d -> p t d", p=P)).then_inc(ld_x, 16)

            def load_c(b, again):
                if again:
                    wait(sp, "pe_b", b - 1, "cv1")
                sp.dma_start(c_T[:], cT[b]).then_inc(ld_c, 16)

            PARTS = (("q", scr_q, st_q, q_st, (0, 1, 0)), ("k", scr_k, st_k, k_st, (0, 0, 1)))

            def write_pairs(b, again):
                for w, (name, written, loaded, _, _) in enumerate(PARTS):
                    wait_all(sp, (sems["act_x"], at("act_x", b, name + "_hi")), *([(loaded, 48 * b)] if again else []))
                    sp.dma_start(scr[w][0].rearrange("(m p) c -> p m c", p=P), qk_hi[w][:].bitcast(F32)).then_inc(written, 16)
                    wait(sp, "dve_x", b, name + "_lo")
                    sp.dma_start(scr[w][1].rearrange("(m p) c -> p m c", p=P), qk_lo[w][:].bitcast(F32)).then_inc(written, 16)

            def read_stacks(b, again):
                for w, (name, written, loaded, st, order) in enumerate(PARTS):
                    wait_all(sp, (written, 32 * b + 32), *([(sems["pe_a"], at("pe_a", b - 1, "s5"))] if again else []))
                    for i, part in enumerate(order):
                        sp.dma_start(st[HD * i:HD * i + HD].bitcast(F32),
                                     scr[w][part].rearrange("(h r) c -> r h c", r=HD)).then_inc(loaded, 16)

            def shift_row(b):
                wait(sp, "act_a", b, "mt")
                row = q_st[R_MAX:R_ALL].bitcast(F32)
                sp.dma_start(row, shift[:].bitcast(F32)).then_inc(ld_shift, 16)

            def store(b):
                wait(sp, "dve_c", b, "out1")
                sp.dma_start(out[b].rearrange("(t p) d -> p t d", p=P), y_n[:]).then_inc(stored, 16)

            sp.dma_start(ident_f, ident_in).then_inc(ld_const, 16)
            sp.dma_start(mask_f.rearrange("p (i c) -> p i c", i=2), mask_in).then_inc(ld_const, 16)
            load_x(0, False)
            for n, (src, dst, raw) in enumerate(WEIGHTS[:3]):
                sp.dma_start(raw, src.rearrange("p k n -> p (k n)")).then_inc(ld_w[n], 16)
            for c in range(2):
                sp.dma_start(alibi_stage[c][R_AUG:R_ALL, :], alibi_in[:, c]).then_inc(ld_alibi, 16)
            sp.dma_start(WEIGHTS[3][2], xwq.rearrange("p k n -> p (k n)")).then_inc(ld_w[3], 16)
            load_xn(0, False)
            sp.dma_start(bo_b[:], bo.partition_broadcast(P)).then_inc(ld_bias, 16)
            sp.dma_start(fb_b[:], fb.partition_broadcast(P)).then_inc(ld_bias, 16)
            load_c(0, False)
            for src, dst in PLAIN[:3]:
                sp.dma_start(dst[:], src).then_inc(ld_plain, 16)
            write_pairs(0, False)
            read_stacks(0, False)
            load_x(1, True)
            sp.wait_ge(set_dve, N_SET)
            sp.wait_ge(w_split, 4)
            sp.dma_start(PLAIN[3][1][:], PLAIN[3][0]).then_inc(ld_plain, 16)
            for n, src in enumerate((fa1, fwT, fa2)):
                sp.dma_start(stage[0][:, n * 512:(n + 1) * 512], src.rearrange("p k n -> p (k n)")).then_inc(ld_ffn, 16)

            def iteration(i, stages="XABC"):
                if "C" in stages:
                    store(i - 1)
                if "A" in stages:
                    shift_row(i + 1)
                if "B" in stages and "A" in stages:
                    load_c(i + 1, True)
                if "X" in stages:
                    if not (isinstance(i, int) and i == NB - 3):
                        load_x(i + 3, True)
                    write_pairs(i + 2, True)
                    read_stacks(i + 2, True)
                    load_xn(i + 2, True)

            iteration(-1, "XA")
            iteration(0, "XAB")
            with sp.Fori(1, NB - 3) as i:
                iteration(i)
            iteration(NB - 3)
            iteration(NB - 2, "ABC")
            store(NB - 2)
            store(NB - 1)
            sp.wait_ge(stored, 16 * NB)

        @block.tensor
        def _(pe):
            def product(dst, lhs, rhs, ks, first=True, last=True):
                n = 0
                for k in ks:
                    for a, c in ((0, 0), (1, 0), (0, 1)):
                        mm = nc.tensor.matmul(dst, lhs(a, k), rhs(c, k), start=(first and n == 0),
                                              stop=(last and n == 3 * len(ks) - 1))
                        n += 1
                return mm

            X = (x_hi, x_lo)
            X1 = (x1_hi, x1_lo)
            X2 = (x2_hi, x2_lo)

            def product_f32(dst, lhs, rhs, ks):
                for k in ks:
                    mm = nc.tensor.matmul(dst, lhs(k), rhs(k), start=(k == 0), stop=(k == len(ks) - 1))
                return mm

            def x_step(fill, b, again):
                if fill != "qk":
                    return
                S = slot("X", fill)
                wait(pe, "act_x", b, "x_hi")
                wait(pe, "pool_x", b, "x_lo")
                if again:
                    wait(pe, "act_a", b - 1, "e1")
                for w, wt in enumerate((w_q, w_k)):
                    for m in range(KD):
                        mm = product(S[:, w, m * T:(m + 1) * T], lambda p, k: wt[p][:, k, m * P:(m + 1) * P],
                                     lambda p, k: X[p][:, k, :], range(KD))
                mm.then_inc(sems["pe_x"], 1)

            def a(fill, b, again):
                S = slot("A", fill)
                if fill == "v":
                    wait(pe, "dve_a", b, "m1")
                    for t in range(NT):
                        mm = product(S[:, 0, t * D:(t + 1) * D], lambda p, k: X[p][:, k, t * P:(t + 1) * P],
                                     lambda p, k: w_v[p][:, k, :], range(KD))
                elif fill[0] == "n":
                    n = int(fill[1])
                    if n == 0:
                        if again:
                            wait(pe, "dve_a", b - 1, "out1")
                        else:
                            wait(pe, "act_x", b, "k_hi")
                            wait(pe, "dve_x", b, "k_lo")
                        pe.wait_ge(st_q, 48 * b + 48)
                        pe.wait_ge(st_k, 48 * b + 48)
                    elif n == 1:
                        if again:
                            wait(pe, "dve_a", b - 1, "add")
                        else:
                            wait(pe, "act_x", b, "k_hi")
                            wait(pe, "dve_x", b, "k_lo")
                    elif n == 4:
                        wait(pe, "act_a", b, "v")
                    else:
                        wait(pe, "dve_a", b, f"m{(0, 2, None, 3)[n - 2]}")
                    per = 4 if n < 2 else 2
                    keys = P if n < 2 else T
                    qt = slice(0, P) if n < 2 else slice(P, T)
                    for bank in range(2):
                        for j in range(per):
                            h = (n * 8 if n < 2 else (n - 2) * 4) + bank * per + j
                            nc.tensor.matmul(S[:, bank, j * keys:(j + 1) * keys], q_st[0:R_MAX, h, qt],
                                             k_st[0:R_MAX, h, 0:keys], start=(j == 0), stop=True, skip_group_check=True)
                        diag = S[:, bank, :].rearrange("p (j c) -> p j c", j=per)[:, :, keys - P:keys]
                        mm = nc.tensor.matmul(diag, ident_b[:], mask_b[:, 0, 0:per, :], start=False, stop=True,
                                              skip_group_check=True)
                elif fill == "mt":
                    wait(pe, "dve_a", b, "m5")
                    for t in range(NT):
                        mm = nc.tensor.transpose(S[0:H, 0, t * P:(t + 1) * P], nmax[:, t, :], ident)
                elif fill[0] == "s":
                    n = int(fill[1])
                    kind, g = S_BLOCKS[n]
                    if n == 0:
                        pe.wait_ge(ld_shift, 16 * b + 16)
                    elif n == 1:
                        wait(pe, "act_a", b, "mt")
                    elif n == 5:
                        wait(pe, "dve_a", b, "out0")
                    else:
                        wait(pe, "act_a", b, f"e{(0, 2, 3)[n - 2]}")
                    per = 2 if kind == "old" else 4
                    keys = slice(0, P) if kind == "old" else slice(P, T)
                    qs = slice(0, T) if kind == "old" else slice(P, T)
                    nq = T if kind == "old" else P
                    for bank in range(2):
                        for j in range(per):
                            h = g * 2 * per + bank * per + j
                            nc.tensor.matmul(S[:, bank, j * nq:(j + 1) * nq], k_st[0:R_ALL, h, keys],
                                             q_st[0:R_ALL, h, qs], start=(j == 0), stop=True, skip_group_check=True)
                        diag = S[:, bank, :].rearrange("p (j c) -> p j c", j=per)[:, :, 0:P]
                        mm = nc.tensor.matmul(diag, ident_b[:], mask_b[:, 1, 0:per, :], start=False, stop=True,
                                              skip_group_check=True)
                elif fill[0] == "o":
                    n = int(fill[1])
                    wait(pe, "act_a", b, f"e{3 * n + 2}")
                    if n == 0 and not (isinstance(b, int) and b == NB - 1):
                        wait(pe, "act_x", b + 1, "k_hi")
                        wait(pe, "dve_x", b + 1, "k_lo")
                    for g in range(2):
                        for j in range(4):
                            h = 8 * n + 4 * g + j
                            nc.tensor.matmul(S[SLOT * j:SLOT * j + SLOT, 0, g * T:(g + 1) * T], v_s[:, 0, h, :],
                                             p_old[:, g, j, :], start=True, stop=True, tile_position=(0, SLOT * j))
                        for j in range(4):
                            h = 8 * n + 4 * g + j
                            mm = nc.tensor.matmul(S[SLOT * j:SLOT * j + SLOT, 0, g * T + P:(g + 1) * T], v_s[:, 1, h, :],
                                                  p_new[:, 4 * g + j, :], start=False, stop=True,
                                                  tile_position=(0, SLOT * j), skip_group_check=True)
                elif fill == "wo":
                    wait(pe, "dve_a", b, "out1")
                    for t in range(NT):
                        mm = product_f32(S[:, 0, t * D:(t + 1) * D], lambda k: o_s[:, k, t * P:(t + 1) * P],
                                         lambda k: w_o[:, k, :], range(H // 4))
                mm.then_inc(sems["pe_a"], 1)

            def b_(fill, b, again):
                S = slot("B", fill)
                if fill in NO_FILL:
                    return
                if fill == "ck":
                    pe.wait_ge(ld_c, 16 * b + 16)
                    if again:
                        wait(pe, "dve_b", b - 1, "out3")
                    else:
                        pe.wait_ge(ld_plain, 16 * len(PLAIN))
                    for m in range(MX):
                        mm = product_f32(S[:, m // 4, (m % 4) * NK:(m % 4 + 1) * NK],
                                         lambda k: w_xk[:, k, m * P:(m + 1) * P], lambda k: c_T[:, k, :], range(KC))
                elif fill in ("cv0", "cv1"):
                    n = int(fill[2])
                    if n == 0:
                        wait(pe, "act_b", b, "q1")
                        wait(pe, "dve_b", b, "q_lo1")
                    else:
                        wait(pe, "dve_b", b, "m1")
                    mm = product_f32(S[0:NK, 0, :], lambda k: c_T[:, k, :],
                                     lambda k: w_xv[:, k, n * 512:(n + 1) * 512], range(KC))
                elif fill == "x1t":
                    wait(pe, "dve_b", b, "norm1")
                    if again:
                        wait(pe, "act_c", b - 1, "y_hi")
                        wait(pe, "dve_c", b - 1, "y_lo")
                    for t in range(NT):
                        for k in range(KD):
                            mm = nc.tensor.transpose(S[:, 0, k * T + t * P:k * T + (t + 1) * P],
                                                     x1[:, t, k * P:(k + 1) * P], ident)
                elif fill in ("cq0", "cq1"):
                    n = int(fill[2])
                    if n == 0:
                        wait(pe, "act_b", b, "x_hi")
                        wait(pe, "dve_b", b, "x_lo")
                        if again:
                            wait(pe, "dve_c", b - 1, "bias")
                        else:
                            wait(pe, "dve_b", b, "k_lo1")
                    for m in range(4):
                        mm = product(S[:, m // 2, (m % 2) * T:(m % 2 + 1) * T],
                                     lambda p, k: w_xq[p][:, k, (4 * n + m) * P:(4 * n + m + 1) * P],
                                     lambda p, k: X1[p][:, k, :], range(KD))
                elif fill[0] == "n":
                    n = int(fill[1])
                    half_, t = n // 2, n % 2
                    if n == 0:
                        wait(pe, "act_b", b, "q0")
                        wait(pe, "dve_b", b, "q_lo0")
                    elif n == 2:
                        wait(pe, "act_b", b, "q1")
                        wait(pe, "act_b", b, "v0")
                    else:
                        wait(pe, "dve_b", b, f"m{(0, None, 2)[n - 1]}")
                    for m in range(4):
                        mm = nc.tensor.matmul(S[:, m // 2, (m % 2) * 2 * NK:(m % 2 + 1) * 2 * NK],
                                              cq[0][:, 4 * half_ + m, t * P:(t + 1) * P],
                                              ck[0][:, 4 * half_ + m].rearrange("p j c -> p (j c)"),
                                              start=True, stop=True)
                elif fill == "mt":
                    wait(pe, "dve_b", b, "m3")
                    wait(pe, "act_b", b, "v1")
                    for t in range(NT):
                        mm = nc.tensor.transpose(S[0:H, 0, t * P:(t + 1) * P], nmax_x[:, t, :], ident)
                elif fill[0] == "s":
                    n = int(fill[1])
                    wait(pe, "act_b", b, ("mt", "mt", "e1", "e2")[n])
                    for j in range(4):
                        h = 4 * n + j
                        dst = S[0:NK, j // 2, (j % 2) * T:(j % 2 + 1) * T]
                        product(dst, lambda p, k: ck[p][:, h // 2, h % 2, :], lambda p, k: cq[p][:, h // 2, :], (0,),
                                last=False)
                        mm = nc.tensor.matmul(dst, ident_r[:, h:h + 1].to_broadcast([P, NK]), shift_x[:],
                                              start=False, stop=True)
                elif fill[0] == "o":
                    n = int(fill[1])
                    wait(pe, "act_b", b, f"e{n}")
                    if n in (1, 2):
                        wait(pe, "dve_b", b, f"out{n - 1}")
                    for part in range(3):
                        for j in range(4):
                            h = 4 * n + j
                            if part < 2:
                                wt = cv[:, h * DX + part * SLOT:h * DX + (part + 1) * SLOT]
                                dst = S[SLOT * j:SLOT * j + SLOT, 0, part * T:(part + 1) * T]
                            else:
                                wt = ones[0:NK, :]
                                dst = S[SLOT * j:SLOT * j + SLOT, 1, 0:T]
                            mm = nc.tensor.matmul(dst, wt, p_x[:, n % 2, j, :], start=True, stop=True,
                                                  tile_position=(0, SLOT * j))
                elif fill == "wo":
                    wait(pe, "dve_b", b, "out3")
                    for t in range(NT):
                        mm = product_f32(S[:, 0, t * D:(t + 1) * D],
                                         lambda k: o_x[:, k // 2, k % 2, t * P:(t + 1) * P],
                                         lambda k: w_xo[:, k, :], range(MX))
                mm.then_inc(sems["pe_b"], 1)

            def c_(fill, b, again):
                S = slot("C", fill)
                if fill == "x2t":
                    wait(pe, "dve_c", b, "norm1")
                    for t in range(NT):
                        for k in range(KD):
                            mm = nc.tensor.transpose(S[:, 0, k * T + t * P:k * T + (t + 1) * P],
                                                     x2[:, t, k * P:(k + 1) * P], ident)
                elif fill == "ff":
                    wait(pe, "act_c", b, "y_hi")
                    wait(pe, "dve_c", b, "y_lo")
                    if not (isinstance(b, int) and b == NB - 1):
                        wait(pe, "act_b", b + 1, "k_hi1")
                        wait(pe, "dve_b", b + 1, "k_lo1")
                    for t in range(NT):
                        mm = product(S[:, 0, t * D:(t + 1) * D], lambda p, k: X2[p][:, k, t * P:(t + 1) * P],
                                     lambda p, k: w_f[p][:, k, :], range(KD))
                else:
                    return
                mm.then_inc(sems["pe_c"], 1)

            def ffn_weight():
                F = ps["B"][0]
                raw = stage[0][:, 0:1536].rearrange("p (w k n) -> p w k n", w=3, k=KD)
                pe.wait_ge(ld_ffn, 48)
                for m in range(KD):
                    for k in range(KD):
                        mm = nc.tensor.matmul(F[:, 0, m * D:(m + 1) * D], raw[:, 0, k, m * P:(m + 1) * P],
                                              raw[:, 1, k, :], start=(k == 0), stop=(k == KD - 1))
                mm.then_inc(set_pe, 1)
                pe.wait_ge(set_dve, N_SET + 1)
                for m in range(KD):
                    for k in range(KD):
                        mm = nc.tensor.matmul(F[:, 1, m * D:(m + 1) * D], r2[:, k, m * P:(m + 1) * P],
                                              raw[:, 2, k, :], start=(k == 0), stop=(k == KD - 1))
                mm.then_inc(set_pe, 1)
                pe.wait_ge(set_dve, N_SET + 3)

            pe.wait_ge(w_split, 3)
            pe.wait_ge(set_dve, N_SET)
            pe.wait_ge(set_pool, N_SET_POOL)
            run_iterations(pe, x_step, a, b_, c_, ffn_weight)

        @block.scalar
        def _(act):
            def x_step(fill, b, again):
                s = sems["act_x"]
                if fill == "x":
                    act.wait_ge(ld_xT, 16 * b + 16)
                    if again:
                        wait(act, "pe_a", b - 1, "v")
                    nc.scalar.copy(x_hi[:], x_T[:]).then_inc(s, 1)
                else:
                    wait(act, "pe_x", b, "qk")
                    if again:
                        act.wait_ge(scr_k, 32 * b)
                        act.wait_ge(scr_q, 32 * b)
                    for w in range(2):
                        nc.scalar.copy(qk_hi[w][:].rearrange("p m c -> p (m c)"), slot("X", fill)[:, w, :]).then_inc(s, 1)

            def a(fill, b, again):
                S = slot("A", fill)
                s = sems["act_a"]
                if fill == "v":
                    wait(act, "pe_a", b, "v")
                    if again:
                        wait(act, "pe_a", b - 1, "o1")
                    nc.scalar.copy(v_s[:, :, :, 0:HD], S[:, 0, :].rearrange("p (t h d) -> p t h d", t=NT, h=H)).then_inc(s, 1)
                elif fill == "mt":
                    wait(act, "pe_a", b, "mt")
                    if again:
                        act.wait_ge(ld_shift, 16 * b)
                    nc.scalar.copy(shift[:], S[0:H, 0, 0:T]).then_inc(s, 1)
                elif fill[0] == "s":
                    n = int(fill[1])
                    kind, g = S_BLOCKS[n]
                    wait(act, "pe_a", b, fill)
                    if n in (3, 4):
                        wait(act, "pe_a", b, "o0")
                    elif n == 0 and again:
                        wait(act, "pe_a", b - 1, "o1")
                    if kind == "old":
                        dst = p_old[:, g % 2].rearrange("p j c -> p (j c)")
                    else:
                        dst = p_new[:].rearrange("p j c -> p (j c)")
                    nc.scalar.activation(dst, S[:].rearrange("p k c -> p (k c)"), ACT.Exp, scale=HD ** -0.5).then_inc(s, 1)

            def b_(fill, b, again):
                S = slot("B", fill)
                s = sems["act_b"]
                if fill == "ck":
                    wait(act, "pe_b", b, "ck")
                    if again:
                        wait(act, "pe_b", b - 1, "s3")
                    for bank in range(2):
                        for j in range(2):
                            ins = nc.scalar.activation(ck[0][:, 4 * bank:4 * bank + 4, j, :],
                                                       S[:, bank, 0:4 * NK].rearrange("p (m c) -> p m c", m=4), ACT.Copy,
                                                       scale=own_rows[:, j:j + 1])
                        ins.then_inc(s, 1)
                elif fill in ("cv0", "cv1"):
                    n = int(fill[2])
                    wait(act, "pe_b", b, fill)
                    if again:
                        wait(act, "pe_b", b - 1, "o3")
                    nc.scalar.copy(cv[:, n * 512:(n + 1) * 512], S[0:NK, 0, :]).then_inc(s, 1)
                elif fill == "x1t":
                    wait(act, "pe_b", b, "x1t")
                    if again:
                        wait(act, "pe_c", b - 1, "ff")
                    nc.scalar.copy(x1_hi[:].rearrange("p k c -> p (k c)"), S[:, 0, :]).then_inc(s, 1)
                elif fill in ("cq0", "cq1"):
                    n = int(fill[2])
                    wait(act, "pe_b", b, fill)
                    if again:
                        wait(act, "pe_b", b - 1, "s3")
                    nc.scalar.copy(cq[0][:, 4 * n:4 * n + 4].rearrange("p (k m) c -> p k (m c)", k=2), S[:]).then_inc(s, 1)
                elif fill == "mt":
                    wait(act, "pe_b", b, "mt")
                    nc.scalar.copy(shift_x[0:H, :], S[0:H, 0, 0:T]).then_inc(s, 1)
                elif fill[0] == "s":
                    n = int(fill[1])
                    wait(act, "pe_b", b, fill)
                    if n >= 2:
                        wait(act, "pe_b", b, f"o{n - 2}")
                    nc.scalar.activation(p_x[:, n % 2].rearrange("p j c -> p (j c)"),
                                         S[0:NK].rearrange("p k c -> p (k c)"), ACT.Exp, scale=DX ** -0.5).then_inc(s, 1)

            def c_(fill, b, again):
                S = slot("C", fill)
                s = sems["act_c"]
                if fill == "x2t":
                    wait(act, "pe_c", b, "x2t")
                    nc.scalar.copy(x2_hi[:].rearrange("p k c -> p (k c)"), S[:, 0, :]).then_inc(s, 1)
                elif fill == "ff":
                    wait(act, "dve_c", b, "bias")
                    nc.scalar.activation(h_f[:], h_f[:], ACT.Tanh).then_inc(s, 1)

            nc.scalar.preload_act_table(ACT.Exp)
            act.wait_ge(set_pool, N_SET_POOL)
            for n, (src, dst, raw) in enumerate(WEIGHTS):
                act.wait_ge(ld_w[n], 16)
                nc.scalar.copy(dst[0][:].rearrange("p k n -> p (k n)"), raw).then_inc(w_hi_done, 1)
            run_iterations(act, x_step, a, b_, c_)

        @block.vector
        def _(dve):
            def layer_stats(res, S, skip, stats, mv, name, b, add, stat, aggr):
                s = sems[name]
                nc.vector.tensor_tensor(res[:].rearrange("p t d -> p (t d)"), S, skip[:].rearrange("p t d -> p (t d)"),
                                        ALU.add).then_inc(s, 1)
                wait(dve, name, b, add)
                for t in range(NT):
                    nc.vector.bn_stats(stats[:, t, :], res[:, t, :]).then_inc(s, 1)
                for t in range(NT):
                    wait_apart(dve, (name, b, f"{stat}{t}"))
                    nc.vector.bn_aggr(mv[:, t, :], stats[:, t, :]).then_inc(s, 1)

            def normalise(dst, res, mv, rstd, name):
                for t in range(NT):
                    nc.vector.tensor_scalar(dst[:, t, :], res[:, t, :], mv[:, t, 0:1], rstd[:, t:t + 1], ALU.subtract,
                                            ALU.mult).then_inc(sems[name], 1)

            def x_step(fill, b, again):
                if fill != "qk":
                    return
                for w, name in enumerate(("q_hi", "k_hi")):
                    wait(dve, "act_x", b, name)
                    if again:
                        dve.wait_ge((scr_q, scr_k)[w], 32 * b)
                    nc.vector.tensor_tensor(qk_lo[w][:].rearrange("p m c -> p (m c)"), slot("X", fill)[:, w, :],
                                            qk_hi[w][:].bitcast(F32).rearrange("p m c -> p (m c)"),
                                            ALU.subtract).then_inc(sems["dve_x"], 1)

            def a(fill, b, again):
                S = slot("A", fill)
                s = sems["dve_a"]
                if fill[0] == "n":
                    n = int(fill[1])
                    wait(dve, "pe_a", b, fill)
                    if n == 0 and again:
                        wait(dve, "pe_a", b - 1, "mt")
                    if n < 2:
                        src = S[:].rearrange("p k (j c) -> p (k j) c", c=P)
                        dst = nmax[:, 0, 8 * n:8 * n + 8]
                    else:
                        src = S[:].rearrange("p k (j c) -> p (k j) c", c=T)
                        dst = nmax[:, 1, 4 * (n - 2):4 * (n - 2) + 4]
                    nc.vector.tensor_reduce(dst, src, AX.X, ALU.max, negate=True).then_inc(s, 1)
                elif fill[0] == "o":
                    n = int(fill[1])
                    wait(dve, "pe_a", b, fill)
                    flat = den[:].rearrange("p g c -> p (g c)")
                    nc.vector.transpose(turned[:], S[:, 0, :]).then_inc(s, 1)
                    wait(dve, "dve_a", b, f"turn{n}")
                    nc.vector.reciprocal(rec[:], turned[:].rearrange("p (k c) -> p k c", c=SLOT)[:, :, HD]).then_inc(s, 1)
                    wait(dve, "dve_a", b, f"rec{n}")
                    nc.vector.transpose(flat, rec[:].rearrange("p (k o) -> p k o", o=1).to_broadcast([P, 2 * T // SLOT, SLOT]))\
                        .then_inc(s, 1)
                    wait(dve, "dve_a", b, f"den{n}")
                    if again and n == 0:
                        wait(dve, "pe_a", b - 1, "wo")
                    nc.vector.tensor_tensor(o_s[:, 2 * n:2 * n + 2].rearrange("p g c -> p (g c)"), S[:, 0, :], flat,
                                            ALU.mult).then_inc(s, 1)
                elif fill == "wo":
                    wait(dve, "pe_a", b, "wo")
                    dve.wait_ge(ld_x, 16 * b + 16)
                    layer_stats(r1, S[:, 0, :], x_n, st1, mv1, "dve_a", b, "add", "stat", "aggr")

            def b_(fill, b, again):
                S = slot("B", fill)
                s = sems["dve_b"]
                if fill == "xn":
                    wait(dve, "pool_a", b, "rstd")
                    if again:
                        wait(dve, "pe_b", b - 1, "x1t")
                        wait(dve, "pool_b", b - 1, "x1b")
                    normalise(x1, r1, mv1, rs1, "dve_b")
                elif fill == "ck":
                    for bank in range(2):
                        wait(dve, "act_b", b, f"k_hi{bank}")
                        for j in range(2):
                            lo, hi = (ck[p][:, 4 * bank:4 * bank + 4, j, :] for p in (1, 0))
                            ins = nc.vector.scalar_tensor_tensor(lo, S[:, bank, 0:4 * NK].rearrange("p (m c) -> p m c", m=4),
                                                                 own_rows[:, j:j + 1], hi.bitcast(F32), ALU.mult,
                                                                 ALU.subtract)
                        ins.then_inc(s, 1)
                elif fill in ("cq0", "cq1"):
                    n = int(fill[2])
                    wait(dve, "act_b", b, f"q{n}")
                    lo, hi = (cq[p][:, 4 * n:4 * n + 4].rearrange("p (k m) c -> p k (m c)", k=2) for p in (1, 0))
                    nc.vector.tensor_tensor(lo, S[:], hi.bitcast(F32), ALU.subtract).then_inc(s, 1)
                elif fill == "x1t":
                    wait(dve, "act_b", b, "x_hi")
                    nc.vector.tensor_tensor(x1_lo[:].rearrange("p k c -> p (k c)"), S[:, 0, :],
                                            x1_hi[:].bitcast(F32).rearrange("p k c -> p (k c)"),
                                            ALU.subtract).then_inc(s, 1)
                elif fill[0] == "n":
                    n = int(fill[1])
                    wait(dve, "pe_b", b, fill)
                    if again and n == 0:
                        wait(dve, "pe_b", b - 1, "mt")
                    half_, t = n // 2, n % 2
                    nc.vector.tensor_reduce(nmax_x[:, t, 8 * half_:8 * half_ + 8].rearrange("p (k j) -> p k j", k=2),
                                            S[:, :, 0:4 * NK].rearrange("p k (j c) -> p k j c", c=NK), AX.X, ALU.max,
                                            negate=True).then_inc(s, 1)
                elif fill[0] == "o":
                    n = int(fill[1])
                    wait(dve, "pe_b", b, fill)
                    nc.vector.transpose(turned[:, 0:T], S[:, 1, 0:T]).then_inc(s, 1)
                    wait(dve, "dve_b", b, f"turn{n}")
                    nc.vector.reciprocal(rec[:, 0:T // SLOT], turned[:, 0:T].rearrange("p (k c) -> p k c", c=SLOT)[:, :, 0]).then_inc(s, 1)
                    wait(dve, "dve_b", b, f"rec{n}")
                    nc.vector.transpose(den[:, 0, :], rec[:, 0:T // SLOT].rearrange("p (k o) -> p k o", o=1).to_broadcast([P, T // SLOT, SLOT]))\
                        .then_inc(s, 1)
                    wait(dve, "dve_b", b, f"den{n}")
                    if again and n == 0:
                        wait(dve, "pe_b", b - 1, "wo")
                    nc.vector.tensor_tensor(o_x[:, n], S[:, 0, :].rearrange("p (k c) -> p k c", k=2),
                                            den[:, 0, :].rearrange("p (o c) -> p o c", o=1).to_broadcast([P, 2, T]),
                                            ALU.mult).then_inc(s, 1)
                elif fill == "wo":
                    wait(dve, "pe_b", b, "wo")
                    wait(dve, "pool_b", b, "x1b")
                    layer_stats(r2, S[:, 0, :], x1b, st2, mv2, "dve_b", b, "add", "stat", "aggr")

            def c_(fill, b, again):
                S = slot("C", fill)
                s = sems["dve_c"]
                if fill == "xn":
                    wait(dve, "pool_b", b, "rstd")
                    if again:
                        wait(dve, "pe_c", b - 1, "x2t")
                    normalise(x2, r2, mv2, rs2, "dve_c")
                elif fill == "x2t":
                    wait(dve, "act_c", b, "y_hi")
                    nc.vector.tensor_tensor(x2_lo[:].rearrange("p k c -> p (k c)"), S[:, 0, :],
                                            x2_hi[:].bitcast(F32).rearrange("p k c -> p (k c)"),
                                            ALU.subtract).then_inc(s, 1)
                elif fill == "ff":
                    wait(dve, "pe_c", b, "ff")
                    if again:
                        dve.wait_ge(stored, 16 * b)
                    nc.vector.tensor_tensor(h_f[:], S[:, 0, :].rearrange("p (t d) -> p t d", t=NT),
                                            fb_b[:].rearrange("p (o d) -> p o d", o=1).to_broadcast([P, NT, D]),
                                            ALU.add).then_inc(s, 1)
                elif fill == "res":
                    wait(dve, "act_c", b, "tanh")
                    layer_stats(r2, h_f[:].rearrange("p t d -> p (t d)"), x2, st2, mv2, "dve_c", b, "add", "stat", "aggr")
                elif fill == "nrm":
                    wait(dve, "pool_c", b, "rstd")
                    normalise(y_n, r2, mv2, rs2, "dve_c")

            n_set = [0]

            def setup(ins):
                n_set[0] += 1
                ins.then_inc(set_dve, 1)
            setup(nc.vector.memset(k_st[:].bitcast(F32), 0.0))
            dve.wait_ge(ld_const, 32)
            setup(nc.vector.tensor_copy(ident_b[:], ident_f))
            setup(nc.vector.tensor_copy(ident_r[:], ident_f))
            for i in range(2):
                setup(nc.vector.tensor_copy(mask_b[:, i], mask_f[:, i * P:(i + 1) * P]
                                            .rearrange("p (o c) -> p o c", o=1).to_broadcast([P, 4, P])))
            setup(nc.vector.memset(half[:], -0.5))
            setup(nc.vector.memset(ones[:], 1.0))
            setup(nc.vector.memset(v_s[:, :, :, HD:SLOT], 1.0))
            setup(nc.vector.memset(shift_x[:].bitcast(F32), 0.0))
            dve.wait_ge(set_pool, 1)
            setup(nc.vector.memset(q_st[R_AUG:R_ALL].bitcast(F32), 1.0))
            dve.wait_ge(set_dve, 1)
            dve.wait_ge(ld_alibi, 32)
            for c in range(2):
                setup(nc.vector.tensor_copy(k_st[R_AUG:R_ALL, 8 * c:8 * c + 8].rearrange("p h c -> p (h c)"),
                                            alibi_stage[c][R_AUG:R_ALL, :]))
            for n, (src, dst, raw) in enumerate(WEIGHTS):
                dve.wait_ge(w_hi_done, n + 1)
                nc.vector.tensor_tensor(dst[1][:].rearrange("p k n -> p (k n)"), raw,
                                        dst[0][:].bitcast(F32).rearrange("p k n -> p (k n)"), ALU.subtract)\
                    .then_inc(w_split, 1)
            setup(nc.vector.memset(h_f[:, 0, 0:1], 0.0))
            assert n_set[0] == N_SET

            def ffn_weight():
                dve.wait_ge(set_pe, 1)
                setup(nc.vector.tensor_copy(r2[:].rearrange("p k c -> p (k c)"), ps["B"][0][:, 0, :]))
                dve.wait_ge(set_pe, 2)
                setup(nc.vector.tensor_copy(w_f[0][:].rearrange("p k c -> p (k c)"), ps["B"][0][:, 1, :]))
                dve.wait_ge(set_dve, N_SET + 2)
                setup(nc.vector.tensor_tensor(w_f[1][:].rearrange("p k c -> p (k c)"), ps["B"][0][:, 1, :],
                                              w_f[0][:].bitcast(F32).rearrange("p k c -> p (k c)"), ALU.subtract))

            run_iterations(dve, x_step, a, b_, c_, ffn_weight)

        @block.gpsimd
        def _(pool):
            def rstd(mv, ve, rs, name, b, eps_step, aggr):
                s = sems[name]
                nc.gpsimd.tensor_scalar(ve[:], mv[:, :, 1], EPS, None, ALU.add).then_inc(s, 1)
                wait(pool, name, b, eps_step)
                nc.gpsimd.tensor_tensor(rs[:], ve[:], half[:], ALU.pow).then_inc(s, 1)

            def x_step(fill, b, again):
                if fill == "x":
                    wait(pool, "act_x", b, "x_hi")
                    if again:
                        wait(pool, "pe_a", b - 1, "v")
                    nc.gpsimd.tensor_tensor(x_lo[:], x_T[:], x_hi[:].bitcast(F32), ALU.subtract).then_inc(sems["pool_x"], 1)

            def a(fill, b, again):
                if fill == "wo":
                    wait_apart(pool, ("dve_a", b, "aggr1"))
                    rstd(mv1, ve1, rs1, "pool_a", b, "veps", "aggr1")

            def b_(fill, b, again):
                s = sems["pool_b"]
                if fill == "xn":
                    wait(pool, "dve_b", b, "norm1")
                    if again:
                        wait(pool, "dve_b", b - 1, "add")
                    else:
                        pool.wait_ge(ld_bias, 32)
                    nc.gpsimd.tensor_tensor(x1b[:], x1[:], bo_b[:].rearrange("p (o d) -> p o d", o=1).to_broadcast([P, NT, D]),
                                            ALU.add).then_inc(s, 1)
                elif fill == "wo":
                    wait_apart(pool, ("dve_b", b, "aggr1"))
                    rstd(mv2, ve2, rs2, "pool_b", b, "veps", "aggr1")

            def c_(fill, b, again):
                if fill == "res":
                    wait_apart(pool, ("dve_c", b, "aggr1"))
                    rstd(mv2, ve2, rs2, "pool_c", b, "veps", "aggr1")

            nc.gpsimd.memset(q_st[:].bitcast(F32), 0.0).then_inc(set_pool, 1)
            nc.gpsimd.memset(own_rows[:], 0.0).then_inc(set_pool, 1)
            pool.wait_ge(set_pool, 2)
            for j in range(2):
                nc.gpsimd.memset(own_rows[DX * j:DX * j + DX, j:j + 1], 1.0).then_inc(set_pool, 1)
            pool.wait_ge(set_pool, N_SET_POOL)
            pool.wait_ge(set_dve, N_SET)
            run_iterations(pool, x_step, a, b_, c_)


def kernel(x, ctx_768, L0_attn_Wq, L0_attn_Wk, L0_attn_Wv, L0_attn_Wo, L0_xattn_Wq, L0_xattn_Wk, L0_xattn_Wv,
           L0_xattn_Wo, L0_xattn_bo, L0_ffn_weight, L0_ffn_aux_weight1, L0_ffn_aux_weight2, L0_ffn_bias):
    import numpy as np
    import concourse.bacc as bacc
    from concourse.bass_utils import run_bass_kernel_spmd

    def rows(w, p=P):
        w = np.asarray(w)
        return np.ascontiguousarray(w.reshape(-1, p, w.shape[-1]).transpose(1, 0, 2))

    x = np.ascontiguousarray(x)
    nb = x.shape[0]
    wo = np.asarray(L0_attn_Wo).T.reshape(H // 4, 4, HD, D)
    wo_slots = np.zeros((H // 4, 4, SLOT, D), wo.dtype)
    wo_slots[:, :, :HD] = wo
    xwo = np.asarray(L0_xattn_Wo).reshape(4, 4, 2, SLOT, D).transpose(0, 2, 1, 3, 4)
    q, k = np.arange(P)[:, None], np.arange(P)[None, :]
    mask = np.where(np.stack([k <= q, q <= k], 1), 0.0, -1e30).astype(np.float32)
    slopes = np.array([(2.0 ** (-8.0 / H)) ** i for i in range(1, H + 1)], np.float32)
    alibi = (slopes[:, None] * np.arange(T, dtype=np.float32)[None, :]) * np.float32(HD ** 0.5)
    hi = (alibi.view(np.uint32) & np.uint32(0xFFFFF000)).view(np.float32)
    aug = np.stack([hi, alibi - hi, np.ones_like(hi)]).reshape(3, 2, H * T // 2)

    arrays = {
        "xT": x.transpose(0, 2, 1).reshape(nb, KD, P, T).transpose(0, 2, 1, 3),
        "x": x,
        "cT": np.asarray(ctx_768).transpose(0, 2, 1).reshape(nb, KC, PC, NK).transpose(0, 2, 1, 3),
        "wqT": rows(np.asarray(L0_attn_Wq).T), "wkT": rows(np.asarray(L0_attn_Wk).T), "wvT": rows(np.asarray(L0_attn_Wv).T),
        "woS": rows(wo_slots.reshape(-1, D)),
        "xwq": rows(L0_xattn_Wq), "xwk": rows(L0_xattn_Wk, PC), "xwv": rows(L0_xattn_Wv, PC),
        "xwo": rows(xwo.reshape(-1, D)), "bo": np.asarray(L0_xattn_bo),
        "fwT": rows(np.asarray(L0_ffn_weight).T), "fa1": rows(L0_ffn_aux_weight1), "fa2": rows(L0_ffn_aux_weight2),
        "fb": np.asarray(L0_ffn_bias),
        "ident_in": np.eye(P, dtype=np.float32), "mask_in": mask, "alibi_in": aug,
    }
    nc = bacc.Bacc("TRN2", target_bir_lowering=False, num_devices=1)
    feeds, args = {}, []
    for name, a in arrays.items():
        feeds[f"in_{name}"] = np.ascontiguousarray(a)
        args.append(nc.dram_tensor(f"in_{name}", a.shape, mybir.dt.from_np(a.dtype), kind="ExternalInput").ap())
    out = nc.dram_tensor("out", x.shape, F32, kind="ExternalOutput").ap()
    build_layer(nc, *args, out)
    return run_bass_kernel_spmd(nc, [feeds], core_ids=[0]).results[0]["out"]
```

```python
from contextlib import ExitStack

import concourse.bass as bass
from concourse import mybir

F32 = mybir.dt.float32
F32R = mybir.dt.float32r
BF16 = mybir.dt.bfloat16
ALU = mybir.AluOpType
ACT = mybir.ActivationFunctionType
AX = mybir.AxisListType

P = 128
T = 256
D = 256
NT = T // P
KD = D // P
H = 16
HD = D // H
DX = 64
NK = 120
DC = 192
KC = 2
PC = DC // KC
SLOT = 32
MX = H * DX // P
EPS = 1e-5
R_AUG = 96
R_MAX = R_AUG + 2
R_ALL = R_AUG + 3

ORDER = ("A.n0 S.wo A.n1 R.wo S.xn A.n2 R.xn B.cv0 C.x2t A.v X.x A.n3 C.ff B.x1t C.res A.n4 B.ck B.cq0 A.n5 "
         "C.nrm B.cq1 A.mt B.n0 X.qk B.n1 A.s0 B.n2 A.s1 B.n3 A.s2 B.mt B.cv1 B.s0 A.o0 B.s1 A.s3 B.o0 A.s4 "
         "B.s2 B.h0 B.o1 A.s5 B.s3 B.h1 B.o2 B.o3 A.o1 B.h2 B.h3").split()
OFFSET = {"X": 2, "A": 1, "R": 0, "B": 0, "S": -1, "C": -1}
NO_FILL = ("xn", "res", "nrm", "x", "h0", "h1", "h2", "h3")
BY_BANK = ("ck", "cq0", "cq1", "qk")
SLOTS_OF = {"A": "AXR", "B": "BSC"}
FILLS = {k: [s for s in ORDER if s[0] in v and s[2:] not in NO_FILL] for k, v in SLOTS_OF.items()}
LAST_READER = {"X.qk": "dve_x k_lo", "A.v": "act_a v", "A.mt": "act_a mt", "R.wo": "dve_r add", "S.wo": "dve_s add",
               "B.ck": "dve_b k_lo1", "B.x1t": "dve_b x_lo", "B.mt": "act_b mt", "C.x2t": "dve_c y_lo",
               "C.ff": "dve_c bias"}
LAST_READER.update({f"A.n{n}": f"dve_a m{n}" for n in range(6)})
LAST_READER.update({f"A.s{n}": f"act_a e{n}" for n in range(6)})
LAST_READER.update({f"A.o{n}": f"dve_a odd{n}" for n in range(2)})
LAST_READER.update({f"B.n{n}": f"dve_b m{n}" for n in range(4)})
LAST_READER.update({f"B.s{n}": f"act_b e{n}" for n in range(4)})
LAST_READER.update({f"B.o{n}": f"dve_b out{n}" for n in range(4)})
LAST_READER.update({f"B.cq{n}": f"dve_b q_lo{n}" for n in range(2)})
LAST_READER.update({f"B.cv{n}": f"act_b v{n}" for n in range(2)})
S_BLOCKS = [("old", 0), ("old", 1), ("new", 0), ("old", 2), ("old", 3), ("new", 1)]


def steps_of(stage, parts=None):
    steps = [s[2:] for s in ORDER if s[0] == stage]
    if parts is None:
        return [p for s in steps if s not in NO_FILL for p in ([s + "_bank0", s] if s in BY_BANK else [s])]
    return [p for s in steps for p in parts.get(s, "").split()]


STEPS = {
    **{f"pe_{stage.lower()}": steps_of(stage) for stage in OFFSET},
    "act_x": "x_hi q_hi k_hi".split(),
    "dve_x": "q_lo k_lo".split(),
    "pool_x": ["x_lo"],
    "act_a": ["v", "mt"] + [f"e{n}" for n in range(6)],
    "dve_a": [f"m{n}" for n in range(6)] +
             [f"{w}{n}" for n in range(2) for w in ("turn", "rec", "den", "even", "odd", "out")],
    "dve_r": "add stat0 stat1 aggr0 aggr1 norm0 norm1".split(),
    "pool_r": "veps rstd x1b".split(),
    "act_b": steps_of("B", {"ck": "k_hi0 k_hi1", "x1t": "x_hi", "cq0": "q0_bank0 q0", "cq1": "q1_bank0 q1",
                            "cv0": "v0", "cv1": "v1", "mt": "mt",
                            "s0": "e0", "s1": "e1", "s2": "e2", "s3": "e3",
                            **{f"h{n}": f"o_hi{n}" for n in range(4)}}),
    "dve_b": steps_of("B", {"ck": "k_lo0 k_lo1", "x1t": "x_lo", "cq0": "q_lo0_bank0 q_lo0", "cq1": "q_lo1_bank0 q_lo1",
                            **{f"n{n}": f"m{n}" for n in range(4)},
                            **{f"o{n}": f"turn{n} rec{n} den{n} out{n}" for n in range(4)}}),
    "pool_b": [f"o_lo{n}" for n in range(4)],
    "dve_s": "add stat0 stat1 aggr0 aggr1 norm0 norm1".split(),
    "pool_s": "veps rstd".split(),
    "act_c": "y_hi tanh".split(),
    "dve_c": "y_lo bias add stat0 stat1 aggr0 aggr1 out0 out1".split(),
    "pool_c": "veps rstd".split(),
}


def build_layer(nc, xT, x, cT, wqT, wkT, wvT, woS, xwq, xwk, xwv, xwo, bo, fwT, fa1, fa2, fb,
                ident_in, mask_in, alibi_in, out):
    NB = x.shape[0]
    scr = [[nc.dram_tensor(f"scr_{w}_{p}", [D, T], F32).ap() for p in ("hi", "lo")] for w in ("q", "k")]
    with ExitStack() as ctx:
        def sb(name, shape, dt=F32):
            return ctx.enter_context(nc.sbuf_tensor(name, shape, dt))

        def sem(name):
            return ctx.enter_context(nc.semaphore(name))

        ps = {st: [ctx.enter_context(nc.psum_tensor(f"ps_{st}{i}", [P, 2, 512], F32)) for i in range(2)] for st in "AB"}

        def slot(st, fill):
            if fill in NO_FILL:
                return None
            pool = "A" if st in SLOTS_OF["A"] else "B"
            return ps[pool][FILLS[pool].index(f"{st}.{fill}") % 2]

        def pair(name, shape):
            return [sb(f"{name}_hi", shape, F32R), sb(f"{name}_lo", shape, F32R)]
        w_q, w_k, w_v = (pair(n, [P, KD, D]) for n in ("w_q", "w_k", "w_v"))
        w_o = sb("w_o", [P, H // 8, D])
        w_xq = pair("w_xq", [P, KD, H * DX])
        w_xk = sb("w_xk", [PC, KC, H * DX])
        w_xv = sb("w_xv", [PC, KC, H * DX])
        w_xo = pair("w_xo", [P, MX, D])
        w_f = pair("w_f", [P, KD, D])
        ident_r = sb("ident", [P, P], F32R)
        ident = ident_r[:].bitcast(F32)
        ident_b = sb("ident_b", [P, P], BF16)
        mask_b = sb("mask_b", [P, 2, 4, P], BF16)
        ones = sb("ones", [P, SLOT])
        bo_b = sb("bo_b", [P, D])
        fb_b = sb("fb_b", [P, D])

        x_T = sb("x_T", [P, KD, T])
        x_hi = sb("x_hi", [P, KD, T], F32R)
        x_lo = sb("x_lo", [P, KD, T], F32R)
        x_n = sb("x_n", [P, NT, D])
        qk_hi = [sb(f"{w}_hi", [P, KD, T], F32R) for w in "qk"]
        qk_lo = [sb(f"{w}_lo", [P, KD, T], F32R) for w in "qk"]
        q_st = sb("q_st", [P, H, T], F32R)
        k_st = sb("k_st", [P, H, T], F32R)
        v_s = sb("v_s", [P, NT, H, SLOT])
        nmax = sb("nmax", [P, NT, H])
        shift = sb("shift", [H, T], F32R)
        p_old = sb("p_old", [P, 2, 4, T])
        p_new = sb("p_new", [P, 8, P])
        turned = sb("turned", [P, 2 * T])
        rec = sb("rec", [P, 2 * T // SLOT])
        den = sb("den", [P, 2, T])
        o_s = sb("o_s", [P, H // 8, T])
        odd = sb("odd", [P, T])
        value_rows = sb("value_rows", [P, 2])
        r1 = sb("r1", [P, NT, D])
        st1 = sb("st1", [P, NT, 6])
        mv1 = sb("mv1", [P, NT, 2])
        ve1 = sb("ve1", [P, NT])
        rs1 = sb("rs1", [P, NT])
        x1 = sb("x1", [P, NT, D])
        x1b = sb("x1b", [P, NT, D])
        half = sb("half", [P, NT])
        own_rows = sb("own_rows", [P, 2])
        c_T = sb("c_T", [PC, KC, NK])
        ck = pair("ck", [P, MX, 2, NK])
        cv = sb("cv", [NK, H * DX])
        x1_hi = sb("x1_hi", [P, KD, T], F32R)
        x1_lo = sb("x1_lo", [P, KD, T], F32R)
        cq = pair("cq", [P, MX, T])
        nmax_x = sb("nmax_x", [P, NT, H])
        shift_x = sb("shift_x", [P, T], F32R)
        p_x = sb("p_x", [P, 2, 4, T])
        o_x = cq
        r2 = sb("r2", [P, NT, D])
        st2 = sb("st2", [P, NT, 6])
        mv2 = sb("mv2", [P, NT, 2])
        ve2 = sb("ve2", [P, NT])
        rs2 = sb("rs2", [P, NT])
        x2 = sb("x2", [P, NT, D])
        x2_hi, x2_lo = x1_hi, x1_lo
        h_f = sb("h_f", [P, NT, D])
        y_n = h_f
        o_raw = (x2, h_f)
        stage = [p_x[:].rearrange("p n j c -> p (n j c)"), p_old[:].rearrange("p g j c -> p (g j c)")]
        mask_f, ident_f = r1[:, 0, :], r1[:, 1, 0:P + 2]
        alibi_stage = [p_new[:, 0:4].rearrange("p h c -> p (h c)"), p_new[:, 4:8].rearrange("p h c -> p (h c)"),
                       cv[:, 0:512], cv[:, 512:1024], o_s[:].rearrange("p n c -> p (n c)"),
                       w_o[:].rearrange("p n c -> p (n c)"), den[:].rearrange("p n c -> p (n c)"), turned[:]]
        ffn_stage = [x1, x1b, x2]
        xwo_stage = [x1, x1b, x2, h_f]

        sems = {name: sem(name) for name in STEPS}
        ld_xT, ld_x, ld_c = sem("ld_xT"), sem("ld_x"), sem("ld_c")
        ld_const = sem("ld_const")
        ld_plain = sem("ld_plain")
        ld_w = [sem(f"ld_w{n}") for n in range(5)]
        ld_alibi, ld_bias, ld_ffn = sem("ld_alibi"), sem("ld_bias"), sem("ld_ffn")
        w_split = sem("w_split")
        w_hi_done = sem("w_hi_done")
        scr_q, scr_k = sem("scr_q"), sem("scr_k")
        st_half = [sem(f"st_half{n}") for n in range(2)]
        ld_shift = sem("ld_shift")
        stored = sem("stored")
        set_dve, set_pool, set_pe = sem("set_dve"), sem("set_pool"), sem("set_pe")

        def at(name, b, step):
            return b * len(STEPS[name]) + STEPS[name].index(step) + 1

        def wait(eng, name, b, step):
            eng.wait_ge(sems[name], at(name, b, step))

        def wait_all(eng, *waits):
            values = [(q, v if isinstance(v, int) else eng.to_reg(v)) for q, v in waits]
            for q, v in values:
                eng.wait_ge(q, v)

        def wait_apart(eng, *waits):
            values = [(sems[name], at(name, b, step)) for name, b, step in waits]
            values = [(q, v if isinstance(v, int) else eng.to_reg(v)) for q, v in values]
            eng.wait_ge(ld_const, 32)
            for q, v in values:
                eng.wait_ge(q, v)

        PLAIN = [(woS, w_o), (xwk, w_xk), (xwv, w_xv)]
        WEIGHTS = [(wqT, w_q, stage[0][:, 0:512]), (wkT, w_k, stage[0][:, 512:1024]), (wvT, w_v, stage[0][:, 1024:1536]),
                   (xwq, w_xq, stage[1])]
        N_SET = 18
        N_SET_POOL = 5

        block = ctx.enter_context(nc.Block())

        def nothing(fill, b, again):
            pass

        def run_iterations(eng, before={}, **stages):
            def iteration(i):
                for step in ORDER:
                    b = i + OFFSET[step[0]]
                    if not isinstance(i, int):
                        stages[step[0]](step[2:], b, True)
                    elif 0 <= b < NB:
                        stages[step[0]](step[2:], b, b > 0)

            for i in range(-2, 2):
                before.get(i, lambda: None)()
                iteration(i)
            with eng.Fori(2, NB - 2) as i:
                iteration(i)
            iteration(NB - 2)
            iteration(NB - 1)
            iteration(NB)

        @block.sync
        def _(sp):
            def load_x(b, again):
                if again:
                    wait_all(sp, (sems["act_x"], at("act_x", b - 1, "x_hi")), (sems["pool_x"], at("pool_x", b - 1, "x_lo")))
                sp.dma_start(x_T[:], xT[b]).then_inc(ld_xT, 16)

            def load_xn(b, again):
                if again:
                    wait(sp, "dve_r", b - 1, "add")
                sp.dma_start(x_n[:], x[b].rearrange("(t p) d -> p t d", p=P)).then_inc(ld_x, 16)

            def load_c(b, again):
                if again:
                    wait(sp, "pe_b", b - 1, "cv1")
                sp.dma_start(c_T[:], cT[b]).then_inc(ld_c, 16)

            PARTS = (("q", scr_q, q_st, (0, 1, 0)), ("k", scr_k, k_st, (0, 0, 1)))

            def write_pairs(b, again):
                for w, (name, written, _, _) in enumerate(PARTS):
                    wait_all(sp, (sems["act_x"], at("act_x", b, name + "_hi")), *([(st_half[1], 96 * b)] if again else []))
                    sp.dma_start(scr[w][0].rearrange("(m p) c -> p m c", p=P), qk_hi[w][:].bitcast(F32)).then_inc(written, 16)
                    wait(sp, "dve_x", b, name + "_lo")
                    sp.dma_start(scr[w][1].rearrange("(m p) c -> p m c", p=P), qk_lo[w][:].bitcast(F32)).then_inc(written, 16)

            def read_stacks(b, again, half_):
                hs, last = slice(8 * half_, 8 * half_ + 8), ("s2", "s5")[half_]
                for w, (name, written, st, order) in enumerate(PARTS):
                    wait_all(sp, (written, 32 * b + 32), *([(sems["pe_a"], at("pe_a", b - 1, last))] if again else []))
                    for i, part in enumerate(order):
                        sp.dma_start(st[HD * i:HD * i + HD, hs].bitcast(F32),
                                     scr[w][part].rearrange("(h r) c -> r h c", r=HD)[:, hs]).then_inc(st_half[half_], 16)

            def shift_row(b):
                wait(sp, "act_a", b, "mt")
                row = q_st[R_MAX:R_ALL].bitcast(F32)
                sp.dma_start(row, shift[:].bitcast(F32)).then_inc(ld_shift, 16)

            def store(b):
                wait(sp, "dve_c", b, "out1")
                sp.dma_start(out[b].rearrange("(t p) d -> p t d", p=P), y_n[:]).then_inc(stored, 16)

            def load_weight(n):
                sp.dma_start(WEIGHTS[n][2], WEIGHTS[n][0].rearrange("p k n -> p (k n)")).then_inc(ld_w[n], 16)

            load_weight(0)
            load_x(0, False)
            load_weight(1)
            sp.dma_start(ident_f, ident_in).then_inc(ld_const, 16)
            sp.dma_start(mask_f.rearrange("p (i c) -> p i c", i=2), mask_in).then_inc(ld_const, 16)
            for c in range(8):
                sp.dma_start(alibi_stage[c][R_AUG:R_ALL, :], alibi_in[:, c]).then_inc(ld_alibi, 16)
            for raw, src in zip(ffn_stage, (fa1, fwT, fa2)):
                sp.dma_start(raw[:], src).then_inc(ld_ffn, 16)
            load_weight(2)
            load_weight(3)
            write_pairs(0, False)
            sp.wait_ge(set_dve, 1)
            sp.wait_ge(set_pool, 1)
            read_stacks(0, False, 0)
            read_stacks(0, False, 1)
            load_x(1, True)
            load_xn(0, False)
            load_c(0, False)
            for src, dst in PLAIN[1:]:
                sp.dma_start(dst[:], src).then_inc(ld_plain, 16)
            sp.wait_ge(set_pe, 2)
            for n in range(4):
                sp.dma_start(xwo_stage[n][:], xwo[:, 2 * n:2 * n + 2]).then_inc(ld_w[4], 16)
            sp.dma_start(bo_b[:], bo.partition_broadcast(P)).then_inc(ld_bias, 16)
            sp.dma_start(fb_b[:], fb.partition_broadcast(P)).then_inc(ld_bias, 16)
            sp.wait_ge(set_dve, N_SET)
            sp.wait_ge(w_split, 4)
            sp.dma_start(PLAIN[0][1][:], PLAIN[0][0]).then_inc(ld_plain, 16)

            def iteration(i, stages="XABC"):
                if "C" in stages:
                    store(i - 1)
                if "A" in stages:
                    shift_row(i + 1)
                if "B" in stages and "A" in stages:
                    load_c(i + 1, True)
                if "X" in stages:
                    if not (isinstance(i, int) and i == NB - 3):
                        load_x(i + 3, True)
                    write_pairs(i + 2, True)
                    read_stacks(i + 2, True, 0)
                    read_stacks(i + 2, True, 1)
                    load_xn(i + 2, True)

            iteration(-1, "XA")
            iteration(0, "XAB")
            with sp.Fori(1, NB - 3) as i:
                iteration(i)
            iteration(NB - 3)
            iteration(NB - 2, "ABC")
            store(NB - 2)
            store(NB - 1)
            sp.wait_ge(stored, 16 * NB)

        @block.tensor
        def _(pe):
            def product(dst, lhs, rhs, ks, first=True, last=True):
                n = 0
                for k in ks:
                    for a, c in ((0, 0), (1, 0), (0, 1)):
                        mm = nc.tensor.matmul(dst, lhs(a, k), rhs(c, k), start=(first and n == 0),
                                              stop=(last and n == 3 * len(ks) - 1))
                        n += 1
                return mm

            def slot_free(st, fill, b):
                fills = FILLS["A" if st in SLOTS_OF["A"] else "B"]
                pos, i = fills.index(f"{st}.{fill}"), b - OFFSET[st]
                for _ in range(2 * len(fills)):
                    pos -= 2
                    if pos < 0:
                        pos, i = pos + len(fills), i - 1
                    before = i + OFFSET[fills[pos][0]]
                    if not isinstance(before, int) or 0 <= before < NB:
                        name, step = LAST_READER[fills[pos]].split()
                        wait(pe, name, before, step)
                        return

            X = (x_hi, x_lo)
            X1 = (x1_hi, x1_lo)
            X2 = (x2_hi, x2_lo)

            def product_f32(dst, lhs, rhs, ks, first=True, last=True):
                for k in ks:
                    mm = nc.tensor.matmul(dst, lhs(k), rhs(k), start=(first and k == ks[0]),
                                          stop=(last and k == ks[-1]))
                return mm

            def x_step(fill, b, again):
                if fill != "qk":
                    return
                S = slot("X", fill)
                wait(pe, "act_x", b, "x_hi")
                wait(pe, "pool_x", b, "x_lo")
                slot_free("X", fill, b)
                for w, wt in enumerate((w_q, w_k)):
                    for m in range(KD):
                        mm = product(S[:, w, m * T:(m + 1) * T], lambda p, k: wt[p][:, k, m * P:(m + 1) * P],
                                     lambda p, k: X[p][:, k, :], range(KD))
                    mm.then_inc(sems["pe_x"], 1)

            def a(fill, b, again):
                S = slot("A", fill)
                slot_free("A", fill, b)
                if fill == "v":
                    for t in range(NT):
                        mm = product(S[:, 0, t * D:(t + 1) * D], lambda p, k: X[p][:, k, t * P:(t + 1) * P],
                                     lambda p, k: w_v[p][:, k, :], range(KD))
                elif fill[0] == "n":
                    n = int(fill[1])
                    if n < 2:
                        pe.wait_ge(st_half[n], 96 * b + 96)
                    per = 4 if n < 2 else 2
                    keys = P if n < 2 else T
                    qt = slice(0, P) if n < 2 else slice(P, T)
                    for bank in range(2):
                        for j in range(per):
                            h = (n * 8 if n < 2 else (n - 2) * 4) + bank * per + j
                            nc.tensor.matmul(S[:, bank, j * keys:(j + 1) * keys], q_st[0:R_MAX, h, qt],
                                             k_st[0:R_MAX, h, 0:keys], start=(j == 0), stop=True, skip_group_check=True)
                        diag = S[:, bank, :].rearrange("p (j c) -> p j c", j=per)[:, :, keys - P:keys]
                        mm = nc.tensor.matmul(diag, ident_b[:], mask_b[:, 0, 0:per, :], start=False, stop=True,
                                              skip_group_check=True)
                elif fill == "mt":
                    wait(pe, "dve_a", b, "m5")
                    for t in range(NT):
                        mm = nc.tensor.transpose(S[0:H, 0, t * P:(t + 1) * P], nmax[:, t, :], ident)
                elif fill[0] == "s":
                    n = int(fill[1])
                    kind, g = S_BLOCKS[n]
                    if n == 0:
                        pe.wait_ge(ld_shift, 16 * b + 16)
                    per = 2 if kind == "old" else 4
                    keys = slice(0, P) if kind == "old" else slice(P, T)
                    qs = slice(0, T) if kind == "old" else slice(P, T)
                    nq = T if kind == "old" else P
                    for bank in range(2):
                        for j in range(per):
                            h = g * 2 * per + bank * per + j
                            nc.tensor.matmul(S[:, bank, j * nq:(j + 1) * nq], k_st[0:R_ALL, h, keys],
                                             q_st[0:R_ALL, h, qs], start=(j == 0), stop=True, skip_group_check=True)
                        diag = S[:, bank, :].rearrange("p (j c) -> p j c", j=per)[:, :, 0:P]
                        mm = nc.tensor.matmul(diag, ident_b[:], mask_b[:, 1, 0:per, :], start=False, stop=True,
                                              skip_group_check=True)
                elif fill[0] == "o":
                    n = int(fill[1])
                    wait(pe, "act_a", b, f"e{3 * n + 2}")
                    for g in range(2):
                        for j in range(4):
                            h = 8 * n + 4 * g + j
                            nc.tensor.matmul(S[SLOT * j:SLOT * j + SLOT, 0, g * T:(g + 1) * T], v_s[:, 0, h, :],
                                             p_old[:, g, j, :], start=True, stop=True, tile_position=(0, SLOT * j))
                        for j in range(4):
                            h = 8 * n + 4 * g + j
                            mm = nc.tensor.matmul(S[SLOT * j:SLOT * j + SLOT, 0, g * T + P:(g + 1) * T], v_s[:, 1, h, :],
                                                  p_new[:, 4 * g + j, :], start=False, stop=True,
                                                  tile_position=(0, SLOT * j), skip_group_check=True)
                mm.then_inc(sems["pe_a"], 1)

            def r_(fill, b, again):
                if fill == "wo":
                    S = slot("R", fill)
                    slot_free("R", fill, b)
                    for ks, ready in (((0,), "out0"), ((1,), "out1")):
                        wait(pe, "dve_a", b, ready)
                        for t in range(NT):
                            mm = product_f32(S[:, t, 0:D], lambda k: o_s[:, k, t * P:(t + 1) * P],
                                             lambda k: w_o[:, k, :], ks, first=ks[0] == 0, last=ks[-1] == H // 8 - 1)
                    mm.then_inc(sems["pe_r"], 1)

            def b_(fill, b, again):
                S = slot("B", fill)
                if fill in NO_FILL:
                    return
                slot_free("B", fill, b)
                if fill in ("ck", "cv0"):
                    pe.wait_ge(ld_c, 16 * b + 16)
                    if not again:
                        pe.wait_ge(ld_plain, 16 * len(PLAIN))
                if fill == "ck":
                    for m in range(MX):
                        mm = product_f32(S[:, m // 4, (m % 4) * NK:(m % 4 + 1) * NK],
                                         lambda k: w_xk[:, k, m * P:(m + 1) * P], lambda k: c_T[:, k, :], range(KC))
                        if m == MX // 2 - 1:
                            mm.then_inc(sems["pe_b"], 1)
                elif fill in ("cv0", "cv1"):
                    n = int(fill[2])
                    mm = product_f32(S[0:NK, 0, :], lambda k: c_T[:, k, :],
                                     lambda k: w_xv[:, k, n * 512:(n + 1) * 512], range(KC))
                elif fill == "x1t":
                    wait(pe, "dve_r", b, "norm1")
                    for t in range(NT):
                        for k in range(KD):
                            mm = nc.tensor.transpose(S[:, 0, k * T + t * P:k * T + (t + 1) * P],
                                                     x1[:, t, k * P:(k + 1) * P], ident)
                elif fill in ("cq0", "cq1"):
                    n = int(fill[2])
                    if n == 0:
                        wait(pe, "act_b", b, "x_hi")
                        wait(pe, "dve_b", b, "x_lo")
                    for m in range(4):
                        mm = product(S[:, m // 2, (m % 2) * T:(m % 2 + 1) * T],
                                     lambda p, k: w_xq[p][:, k, (4 * n + m) * P:(4 * n + m + 1) * P],
                                     lambda p, k: X1[p][:, k, :], range(KD))
                        if m == 1:
                            mm.then_inc(sems["pe_b"], 1)
                elif fill[0] == "n":
                    n = int(fill[1])
                    half_, t = n // 2, n % 2
                    if n in (0, 2):
                        wait(pe, "act_b", b, f"q{half_}")
                    for m in range(4):
                        mm = nc.tensor.matmul(S[:, m // 2, (m % 2) * 2 * NK:(m % 2 + 1) * 2 * NK],
                                              cq[0][:, 4 * half_ + m, t * P:(t + 1) * P],
                                              ck[0][:, 4 * half_ + m].rearrange("p j c -> p (j c)"),
                                              start=True, stop=True)
                elif fill == "mt":
                    wait(pe, "dve_b", b, "m3")
                    for t in range(NT):
                        mm = nc.tensor.transpose(S[0:H, 0, t * P:(t + 1) * P], nmax_x[:, t, :], ident)
                elif fill[0] == "s":
                    n = int(fill[1])
                    if n == 0:
                        wait(pe, "act_b", b, "mt")
                    for j in range(4):
                        h = 4 * n + j
                        dst = S[0:NK, j // 2, (j % 2) * T:(j % 2 + 1) * T]
                        product(dst, lambda p, k: ck[p][:, h // 2, h % 2, :], lambda p, k: cq[p][:, h // 2, :], (0,),
                                last=False)
                        mm = nc.tensor.matmul(dst, ident_r[:, h:h + 1].to_broadcast([P, NK]), shift_x[:],
                                              start=False, stop=True)
                elif fill[0] == "o":
                    n = int(fill[1])
                    wait(pe, "act_b", b, f"e{n}")
                    for part in range(3):
                        for j in range(4):
                            h = 4 * n + j
                            if part < 2:
                                wt = cv[:, h * DX + part * SLOT:h * DX + (part + 1) * SLOT]
                                dst = S[SLOT * j:SLOT * j + SLOT, 0, part * T:(part + 1) * T]
                            else:
                                wt = ones[0:NK, :]
                                dst = S[SLOT * j:SLOT * j + SLOT, 1, 0:T]
                            mm = nc.tensor.matmul(dst, wt, p_x[0:NK, n % 2, j, :], start=True, stop=True,
                                                  tile_position=(0, SLOT * j))
                mm.then_inc(sems["pe_b"], 1)

            def s_(fill, b, again):
                if fill == "wo":
                    S = slot("S", fill)
                    slot_free("S", fill, b)
                    if not again:
                        pe.wait_ge(w_split, 8)
                    for ks, ready in ((range(0, 6), "o_lo2"), (range(6, 8), "o_lo3")):
                        wait(pe, "pool_b", b, ready)
                        for t in range(NT):
                            mm = product(S[:, t, 0:D], lambda p, k: o_x[p][:, k, t * P:(t + 1) * P],
                                         lambda p, k: w_xo[p][:, k, :], ks, first=ks[0] == 0, last=ks[-1] == MX - 1)
                    mm.then_inc(sems["pe_s"], 1)

            def c_(fill, b, again):
                S = slot("C", fill)
                if fill == "x2t":
                    slot_free("C", fill, b)
                    wait(pe, "dve_s", b, "norm1")
                    for t in range(NT):
                        for k in range(KD):
                            mm = nc.tensor.transpose(S[:, 0, k * T + t * P:k * T + (t + 1) * P],
                                                     x2[:, t, k * P:(k + 1) * P], ident)
                elif fill == "ff":
                    slot_free("C", fill, b)
                    wait(pe, "act_c", b, "y_hi")
                    wait(pe, "dve_c", b, "y_lo")
                    for t in range(NT):
                        mm = product(S[:, 0, t * D:(t + 1) * D], lambda p, k: X2[p][:, k, t * P:(t + 1) * P],
                                     lambda p, k: w_f[p][:, k, :], range(KD))
                else:
                    return
                mm.then_inc(sems["pe_c"], 1)

            def ffn_weight():
                F = ps["B"][0]
                pe.wait_ge(ld_ffn, 48)
                for m in range(KD):
                    for k in range(KD):
                        mm = nc.tensor.matmul(F[:, 0, m * D:(m + 1) * D], ffn_stage[0][:, k, m * P:(m + 1) * P],
                                              ffn_stage[1][:, k, :], start=(k == 0), stop=(k == KD - 1))
                mm.then_inc(set_pe, 1)
                pe.wait_ge(set_dve, N_SET + 1)
                for m in range(KD):
                    for k in range(KD):
                        mm = nc.tensor.matmul(F[:, 1, m * D:(m + 1) * D], r2[:, k, m * P:(m + 1) * P],
                                              ffn_stage[2][:, k, :], start=(k == 0), stop=(k == KD - 1))
                mm.then_inc(set_pe, 1)

            def ffn_weight_ready():
                pe.wait_ge(set_dve, N_SET + 3)

            def constants_ready():
                ffn_weight()
                pe.wait_ge(w_split, 3)
                pe.wait_ge(set_dve, N_SET)
                pe.wait_ge(set_pool, N_SET_POOL)

            pe.wait_ge(w_split, 2)
            run_iterations(pe, {-1: constants_ready, 0: ffn_weight_ready}, X=x_step, A=a, R=r_, B=b_, S=s_, C=c_)

        @block.scalar
        def _(act):
            def x_step(fill, b, again):
                s = sems["act_x"]
                if fill == "x":
                    act.wait_ge(ld_xT, 16 * b + 16)
                    if again:
                        wait(act, "pe_a", b - 1, "v")
                    nc.scalar.copy(x_hi[:], x_T[:]).then_inc(s, 1)
                else:
                    wait(act, "pe_x", b, "qk_bank0")
                    if again:
                        act.wait_ge(scr_k, 32 * b)
                        act.wait_ge(scr_q, 32 * b)
                    for w in range(2):
                        if w == 1:
                            wait(act, "pe_x", b, "qk")
                        nc.scalar.copy(qk_hi[w][:].rearrange("p m c -> p (m c)"), slot("X", fill)[:, w, :]).then_inc(s, 1)

            def a(fill, b, again):
                S = slot("A", fill)
                s = sems["act_a"]
                if fill == "v":
                    wait(act, "pe_a", b, "v")
                    if again:
                        wait(act, "pe_a", b - 1, "o1")
                    for g in range(2):
                        for t in range(NT):
                            ins = nc.scalar.copy(v_s[:, t].rearrange("p (n g j) c -> p n g j c", g=2, j=4)
                                                 [:, :, g, :, HD * g:HD * g + HD],
                                                 S[:, 0, t * D:(t + 1) * D].rearrange("p (n g j d) -> p n g j d", g=2, j=4, d=HD)
                                                 [:, :, g])
                    ins.then_inc(s, 1)
                elif fill == "mt":
                    wait(act, "pe_a", b, "mt")
                    if again:
                        act.wait_ge(ld_shift, 16 * b)
                    nc.scalar.copy(shift[:], S[0:H, 0, 0:T]).then_inc(s, 1)
                elif fill[0] == "s":
                    n = int(fill[1])
                    kind, g = S_BLOCKS[n]
                    wait(act, "pe_a", b, fill)
                    if n in (3, 4):
                        wait(act, "pe_a", b, "o0")
                    elif n == 0 and again:
                        wait(act, "pe_a", b - 1, "o1")
                    if kind == "old":
                        dst = p_old[:, g % 2].rearrange("p j c -> p (j c)")
                    else:
                        dst = p_new[:].rearrange("p j c -> p (j c)")
                    nc.scalar.activation(dst, S[:].rearrange("p k c -> p (k c)"), ACT.Exp, scale=HD ** -0.5).then_inc(s, 1)

            def b_(fill, b, again):
                S = slot("B", fill)
                s = sems["act_b"]
                if fill == "ck":
                    wait(act, "pe_b", b, "ck_bank0")
                    if again:
                        wait(act, "pe_b", b - 1, "s3")
                    for bank in range(2):
                        if bank == 1:
                            wait(act, "pe_b", b, "ck")
                        for j in range(2):
                            ins = nc.scalar.activation(ck[0][:, 4 * bank:4 * bank + 4, j, :],
                                                       S[:, bank, 0:4 * NK].rearrange("p (m c) -> p m c", m=4), ACT.Copy,
                                                       scale=own_rows[:, j:j + 1])
                        ins.then_inc(s, 1)
                elif fill in ("cv0", "cv1"):
                    n = int(fill[2])
                    wait(act, "pe_b", b, fill)
                    if again:
                        wait(act, "pe_b", b - 1, "o3")
                    nc.scalar.copy(cv[:, n * 512:(n + 1) * 512], S[0:NK, 0, :]).then_inc(s, 1)
                elif fill == "x1t":
                    wait(act, "pe_b", b, "x1t")
                    if again:
                        wait(act, "pe_c", b - 1, "ff")
                    nc.scalar.copy(x1_hi[:].rearrange("p k c -> p (k c)"), S[:, 0, :]).then_inc(s, 1)
                elif fill in ("cq0", "cq1"):
                    n = int(fill[2])
                    wait(act, "pe_b", b, fill + "_bank0")
                    if again:
                        wait(act, "pe_s", b - 1, "wo")
                    for bank in range(2):
                        if bank == 1:
                            wait(act, "pe_b", b, fill)
                        m = 4 * n + 2 * bank
                        nc.scalar.copy(cq[0][:, m:m + 2].rearrange("p m c -> p (m c)"), S[:, bank, :]).then_inc(s, 1)
                elif fill[0] == "h":
                    n = int(fill[1])
                    wait(act, "dve_b", b, f"out{n}")
                    nc.scalar.copy(o_x[0][:, 2 * n:2 * n + 2], o_raw[n % 2][:]).then_inc(s, 1)
                elif fill == "mt":
                    wait(act, "pe_b", b, "mt")
                    nc.scalar.copy(shift_x[0:H, :], S[0:H, 0, 0:T]).then_inc(s, 1)
                elif fill[0] == "s":
                    n = int(fill[1])
                    wait(act, "pe_b", b, fill)
                    if n >= 2:
                        wait(act, "pe_b", b, f"o{n - 2}")
                    nc.scalar.activation(p_x[0:NK, n % 2].rearrange("p j c -> p (j c)"),
                                         S[0:NK].rearrange("p k c -> p (k c)"), ACT.Exp, scale=DX ** -0.5).then_inc(s, 1)

            def c_(fill, b, again):
                S = slot("C", fill)
                s = sems["act_c"]
                if fill == "x2t":
                    wait(act, "pe_c", b, "x2t")
                    nc.scalar.copy(x2_hi[:].rearrange("p k c -> p (k c)"), S[:, 0, :]).then_inc(s, 1)
                elif fill == "ff":
                    wait(act, "dve_c", b, "bias")
                    nc.scalar.activation(h_f[:], h_f[:], ACT.Tanh).then_inc(s, 1)

            nc.scalar.preload_act_table(ACT.Exp)

            def split_hi(n):
                act.wait_ge(ld_w[n], 16)
                nc.scalar.copy(WEIGHTS[n][1][0][:].rearrange("p k n -> p (k n)"), WEIGHTS[n][2]).then_inc(w_hi_done, 1)

            def other_weights():
                split_hi(2)
                split_hi(3)
                act.wait_ge(set_pool, N_SET_POOL)

            def output_weights():
                act.wait_ge(ld_w[4], 64)
                for n in range(4):
                    nc.scalar.copy(w_xo[0][:, 2 * n:2 * n + 2], xwo_stage[n][:]).then_inc(w_hi_done, 1)

            split_hi(0)
            split_hi(1)
            run_iterations(act, {-1: other_weights, 0: output_weights}, X=x_step, A=a, R=nothing, B=b_, S=nothing, C=c_)

        @block.vector
        def _(dve):
            def layer_stats(res, S, skip, stats, mv, name, b):
                s = sems[name]
                nc.vector.tensor_tensor(res[:], S, skip[:], ALU.add).then_inc(s, 1)
                wait(dve, name, b, "add")
                for t in range(NT):
                    nc.vector.bn_stats(stats[:, t, :], res[:, t, :]).then_inc(s, 1)
                for t in range(NT):
                    wait_apart(dve, (name, b, f"stat{t}"))
                    nc.vector.bn_aggr(mv[:, t, :], stats[:, t, :]).then_inc(s, 1)

            def normalise(dst, res, mv, rstd, name):
                for t in range(NT):
                    nc.vector.tensor_scalar(dst[:, t, :], res[:, t, :], mv[:, t, 0:1], rstd[:, t:t + 1], ALU.subtract,
                                            ALU.mult).then_inc(sems[name], 1)

            def x_step(fill, b, again):
                if fill != "qk":
                    return
                for w, name in enumerate(("q_hi", "k_hi")):
                    wait(dve, "act_x", b, name)
                    if again:
                        dve.wait_ge((scr_q, scr_k)[w], 32 * b)
                    nc.vector.tensor_tensor(qk_lo[w][:].rearrange("p m c -> p (m c)"), slot("X", fill)[:, w, :],
                                            qk_hi[w][:].bitcast(F32).rearrange("p m c -> p (m c)"),
                                            ALU.subtract).then_inc(sems["dve_x"], 1)

            def a(fill, b, again):
                S = slot("A", fill)
                s = sems["dve_a"]
                if fill[0] == "n":
                    n = int(fill[1])
                    wait(dve, "pe_a", b, fill)
                    if n == 0 and again:
                        wait(dve, "pe_a", b - 1, "mt")
                    if n < 2:
                        src = S[:].rearrange("p k (j c) -> p (k j) c", c=P)
                        dst = nmax[:, 0, 8 * n:8 * n + 8]
                    else:
                        src = S[:].rearrange("p k (j c) -> p (k j) c", c=T)
                        dst = nmax[:, 1, 4 * (n - 2):4 * (n - 2) + 4]
                    nc.vector.tensor_reduce(dst, src, AX.X, ALU.max, negate=True).then_inc(s, 1)
                elif fill[0] == "o":
                    n = int(fill[1])
                    wait(dve, "pe_a", b, fill)
                    flat = den[:].rearrange("p g c -> p (g c)")
                    nc.vector.transpose(turned[:], S[:, 0, :]).then_inc(s, 1)
                    wait(dve, "dve_a", b, f"turn{n}")
                    for g in range(2):
                        ins = nc.vector.reciprocal(rec[:, g * T // SLOT:(g + 1) * T // SLOT],
                                                   turned[:, g * T:(g + 1) * T].rearrange("p (k c) -> p k c", c=SLOT)
                                                   [:, :, HD * (1 - g)])
                    ins.then_inc(s, 1)
                    wait(dve, "dve_a", b, f"rec{n}")
                    nc.vector.transpose(flat, rec[:].rearrange("p (k o) -> p k o", o=1).to_broadcast([P, 2 * T // SLOT, SLOT]))\
                        .then_inc(s, 1)
                    wait(dve, "dve_a", b, f"den{n}")
                    if again and n == 0:
                        wait(dve, "pe_r", b - 1, "wo")
                    for g, (dst, step) in enumerate(((o_s[:, n], "even"), (odd[:], "odd"))):
                        nc.vector.scalar_tensor_tensor(dst, S[:, 0, g * T:(g + 1) * T], value_rows[:, g:g + 1], den[:, g],
                                                       ALU.mult, ALU.mult).then_inc(s, 1)
                    wait(dve, "dve_a", b, f"odd{n}")
                    nc.vector.tensor_tensor(o_s[:, n], o_s[:, n], odd[:], ALU.add).then_inc(s, 1)

            def r_(fill, b, again):
                if fill == "wo":
                    wait(dve, "pe_r", b, "wo")
                    dve.wait_ge(ld_x, 16 * b + 16)
                    layer_stats(r1, slot("R", fill)[:, :, 0:D], x_n, st1, mv1, "dve_r", b)
                elif fill == "xn":
                    wait(dve, "pool_r", b, "rstd")
                    if again:
                        wait(dve, "pe_b", b - 1, "x1t")
                        wait(dve, "pool_r", b - 1, "x1b")
                    normalise(x1, r1, mv1, rs1, "dve_r")

            def b_(fill, b, again):
                S = slot("B", fill)
                s = sems["dve_b"]
                if fill == "ck":
                    for bank in range(2):
                        wait(dve, "act_b", b, f"k_hi{bank}")
                        for j in range(2):
                            lo, hi = (ck[p][:, 4 * bank:4 * bank + 4, j, :] for p in (1, 0))
                            ins = nc.vector.scalar_tensor_tensor(lo, S[:, bank, 0:4 * NK].rearrange("p (m c) -> p m c", m=4),
                                                                 own_rows[:, j:j + 1], hi.bitcast(F32), ALU.mult,
                                                                 ALU.subtract)
                        ins.then_inc(s, 1)
                elif fill in ("cq0", "cq1"):
                    n = int(fill[2])
                    for bank in range(2):
                        wait(dve, "act_b", b, (f"q{n}_bank0", f"q{n}")[bank])
                        m = 4 * n + 2 * bank
                        lo, hi = (cq[p][:, m:m + 2].rearrange("p m c -> p (m c)") for p in (1, 0))
                        nc.vector.tensor_tensor(lo, S[:, bank, :], hi.bitcast(F32), ALU.subtract).then_inc(s, 1)
                elif fill == "x1t":
                    wait(dve, "act_b", b, "x_hi")
                    nc.vector.tensor_tensor(x1_lo[:].rearrange("p k c -> p (k c)"), S[:, 0, :],
                                            x1_hi[:].bitcast(F32).rearrange("p k c -> p (k c)"),
                                            ALU.subtract).then_inc(s, 1)
                elif fill[0] == "n":
                    n = int(fill[1])
                    wait(dve, "pe_b", b, fill)
                    if again and n == 0:
                        wait(dve, "pe_b", b - 1, "mt")
                    half_, t = n // 2, n % 2
                    nc.vector.tensor_reduce(nmax_x[:, t, 8 * half_:8 * half_ + 8].rearrange("p (k j) -> p k j", k=2),
                                            S[:, :, 0:4 * NK].rearrange("p k (j c) -> p k j c", c=NK), AX.X, ALU.max,
                                            negate=True).then_inc(s, 1)
                elif fill[0] == "o":
                    n = int(fill[1])
                    wait(dve, "pe_b", b, fill)
                    nc.vector.transpose(turned[:, 0:T], S[:, 1, 0:T]).then_inc(s, 1)
                    wait(dve, "dve_b", b, f"turn{n}")
                    nc.vector.reciprocal(rec[:, 0:T // SLOT],
                                         turned[:, 0:T].rearrange("p (k c) -> p k c", c=SLOT)[:, :, 0]).then_inc(s, 1)
                    wait(dve, "dve_b", b, f"rec{n}")
                    nc.vector.transpose(den[:, 0, :], rec[:, 0:T // SLOT].rearrange("p (k o) -> p k o", o=1).to_broadcast([P, T // SLOT, SLOT]))\
                        .then_inc(s, 1)
                    wait(dve, "dve_b", b, f"den{n}")
                    if n < 2:
                        if again and n == 1:
                            dve.wait_ge(stored, 16 * b)
                    else:
                        wait(dve, "pool_b", b, f"o_lo{n - 2}")
                    nc.vector.tensor_tensor(o_raw[n % 2][:].rearrange("p t d -> p (t d)").rearrange("p (k c) -> p k c", k=2), S[:, 0, :].rearrange("p (k c) -> p k c", k=2),
                                            den[:, 0, :].rearrange("p (o c) -> p o c", o=1).to_broadcast([P, 2, T]),
                                            ALU.mult).then_inc(s, 1)

            def s_(fill, b, again):
                if fill == "wo":
                    wait(dve, "pe_s", b, "wo")
                    wait(dve, "pool_r", b, "x1b")
                    layer_stats(r2, slot("S", fill)[:, :, 0:D], x1b, st2, mv2, "dve_s", b)
                elif fill == "xn":
                    wait(dve, "pool_s", b, "rstd")
                    if again:
                        wait(dve, "pe_c", b - 1, "x2t")
                    normalise(x2, r2, mv2, rs2, "dve_s")

            def c_(fill, b, again):
                S = slot("C", fill)
                s = sems["dve_c"]
                if fill == "x2t":
                    wait(dve, "act_c", b, "y_hi")
                    nc.vector.tensor_tensor(x2_lo[:].rearrange("p k c -> p (k c)"), S[:, 0, :],
                                            x2_hi[:].bitcast(F32).rearrange("p k c -> p (k c)"),
                                            ALU.subtract).then_inc(s, 1)
                elif fill == "ff":
                    wait(dve, "pe_c", b, "ff")
                    if again:
                        dve.wait_ge(stored, 16 * b)
                    nc.vector.tensor_tensor(h_f[:], S[:, 0, :].rearrange("p (t d) -> p t d", t=NT),
                                            fb_b[:].rearrange("p (o d) -> p o d", o=1).to_broadcast([P, NT, D]),
                                            ALU.add).then_inc(s, 1)
                elif fill == "res":
                    wait(dve, "act_c", b, "tanh")
                    layer_stats(r2, h_f[:], x2, st2, mv2, "dve_c", b)
                elif fill == "nrm":
                    wait(dve, "pool_c", b, "rstd")
                    normalise(y_n, r2, mv2, rs2, "dve_c")

            n_set = [0]

            def setup(ins):
                n_set[0] += 1
                ins.then_inc(set_dve, 1)
            def split_lo(n):
                _, dst, raw = WEIGHTS[n]
                dve.wait_ge(w_hi_done, n + 1)
                nc.vector.tensor_tensor(dst[1][:].rearrange("p k n -> p (k n)"), raw,
                                        dst[0][:].bitcast(F32).rearrange("p k n -> p (k n)"), ALU.subtract)\
                    .then_inc(w_split, 1)

            setup(nc.vector.memset(k_st[:].bitcast(F32), 0.0))
            split_lo(0)
            split_lo(1)
            dve.wait_ge(ld_const, 32)
            setup(nc.vector.tensor_copy(ident_b[:], ident_f[:, 0:P]))
            setup(nc.vector.tensor_copy(ident_r[:], ident_f[:, 0:P]))
            setup(nc.vector.tensor_copy(value_rows[:], ident_f[:, P:P + 2]))
            for i in range(2):
                setup(nc.vector.tensor_copy(mask_b[:, i], mask_f[:, i * P:(i + 1) * P]
                                            .rearrange("p (o c) -> p o c", o=1).to_broadcast([P, 4, P])))
            setup(nc.vector.memset(half[:], -0.5))
            setup(nc.vector.memset(ones[:], 1.0))
            setup(nc.vector.memset(v_s[:], 1.0))
            setup(nc.vector.memset(shift_x[:].bitcast(F32), 0.0))
            dve.wait_ge(set_dve, 1)
            dve.wait_ge(ld_alibi, 128)
            for c in range(8):
                setup(nc.vector.tensor_copy(k_st[R_AUG:R_ALL, 2 * c:2 * c + 2].rearrange("p h c -> p (h c)"),
                                            alibi_stage[c][R_AUG:R_ALL, :]))

            def other_weights():
                split_lo(2)
                split_lo(3)
                assert n_set[0] == N_SET
                ffn_weight()

            def ffn_weight():
                dve.wait_ge(set_pe, 1)
                setup(nc.vector.tensor_copy(r2[:].rearrange("p k c -> p (k c)"), ps["B"][0][:, 0, :]))
                dve.wait_ge(set_pe, 2)
                setup(nc.vector.tensor_copy(w_f[0][:].rearrange("p k c -> p (k c)"), ps["B"][0][:, 1, :]))
                dve.wait_ge(set_dve, N_SET + 2)
                setup(nc.vector.tensor_tensor(w_f[1][:].rearrange("p k c -> p (k c)"), ps["B"][0][:, 1, :],
                                              w_f[0][:].bitcast(F32).rearrange("p k c -> p (k c)"), ALU.subtract))

            def output_weights():
                for n in range(4):
                    dve.wait_ge(w_hi_done, 5 + n)
                    nc.vector.tensor_tensor(w_xo[1][:, 2 * n:2 * n + 2], xwo_stage[n][:],
                                            w_xo[0][:, 2 * n:2 * n + 2].bitcast(F32), ALU.subtract).then_inc(w_split, 1)

            run_iterations(dve, {-1: other_weights, 0: output_weights}, X=x_step, A=a, R=r_, B=b_, S=s_, C=c_)

        @block.gpsimd
        def _(pool):
            def rstd(mv, ve, rs, name, b, eps_step, aggr):
                s = sems[name]
                nc.gpsimd.tensor_scalar(ve[:], mv[:, :, 1], EPS, None, ALU.add).then_inc(s, 1)
                wait(pool, name, b, eps_step)
                nc.gpsimd.tensor_tensor(rs[:], ve[:], half[:], ALU.pow).then_inc(s, 1)

            def x_step(fill, b, again):
                if fill == "x":
                    wait(pool, "act_x", b, "x_hi")
                    if again:
                        wait(pool, "pe_a", b - 1, "v")
                    nc.gpsimd.tensor_tensor(x_lo[:], x_T[:], x_hi[:].bitcast(F32), ALU.subtract).then_inc(sems["pool_x"], 1)

            def r_(fill, b, again):
                if fill == "wo":
                    wait_apart(pool, ("dve_r", b, "aggr1"))
                    rstd(mv1, ve1, rs1, "pool_r", b, "veps", "aggr1")
                elif fill == "xn":
                    wait(pool, "dve_r", b, "norm1")
                    if again:
                        wait(pool, "dve_s", b - 1, "add")
                    else:
                        pool.wait_ge(ld_bias, 32)
                    nc.gpsimd.tensor_tensor(x1b[:], x1[:], bo_b[:].rearrange("p (o d) -> p o d", o=1).to_broadcast([P, NT, D]),
                                            ALU.add).then_inc(sems["pool_r"], 1)

            def b_(fill, b, again):
                if fill[0] == "h":
                    n = int(fill[1])
                    wait(pool, "act_b", b, f"o_hi{n}")
                    lo, hi = (o_x[p][:, 2 * n:2 * n + 2] for p in (1, 0))
                    nc.gpsimd.tensor_tensor(lo, o_raw[n % 2][:], hi.bitcast(F32), ALU.subtract).then_inc(sems["pool_b"], 1)

            def s_(fill, b, again):
                if fill == "wo":
                    wait_apart(pool, ("dve_s", b, "aggr1"))
                    rstd(mv2, ve2, rs2, "pool_s", b, "veps", "aggr1")

            def c_(fill, b, again):
                if fill == "res":
                    wait_apart(pool, ("dve_c", b, "aggr1"))
                    rstd(mv2, ve2, rs2, "pool_c", b, "veps", "aggr1")

            nc.gpsimd.memset(q_st[:].bitcast(F32), 0.0).then_inc(set_pool, 1)
            nc.gpsimd.memset(own_rows[:], 0.0).then_inc(set_pool, 1)
            pool.wait_ge(set_pool, 2)
            for j in range(2):
                nc.gpsimd.memset(own_rows[DX * j:DX * j + DX, j:j + 1], 1.0).then_inc(set_pool, 1)
            pool.wait_ge(set_pool, 4)

            def ones_rows():
                wait(pool, "pool_x", 0, "x_lo")
                nc.gpsimd.memset(q_st[R_AUG:R_ALL].bitcast(F32), 1.0).then_inc(set_pool, 1)
                pool.wait_ge(set_pool, N_SET_POOL)
                pool.wait_ge(set_dve, N_SET)

            run_iterations(pool, {-1: ones_rows}, X=x_step, A=nothing, R=r_, B=b_, S=s_, C=c_)


def kernel(x, ctx_768, L0_attn_Wq, L0_attn_Wk, L0_attn_Wv, L0_attn_Wo, L0_xattn_Wq, L0_xattn_Wk, L0_xattn_Wv,
           L0_xattn_Wo, L0_xattn_bo, L0_ffn_weight, L0_ffn_aux_weight1, L0_ffn_aux_weight2, L0_ffn_bias):
    import numpy as np
    import concourse.bacc as bacc
    from concourse.bass_utils import run_bass_kernel_spmd

    def rows(w, p=P):
        w = np.asarray(w)
        return np.ascontiguousarray(w.reshape(-1, p, w.shape[-1]).transpose(1, 0, 2))

    x = np.ascontiguousarray(x)
    nb = x.shape[0]
    q, k = np.arange(P)[:, None], np.arange(P)[None, :]
    wo = np.asarray(L0_attn_Wo).T.reshape(H // 8, 2, 4, HD, D).transpose(0, 2, 1, 3, 4)
    in_even = (q % SLOT < HD).astype(np.float32)
    xwo = np.asarray(L0_xattn_Wo).reshape(4, 4, 2, SLOT, D).transpose(0, 2, 1, 3, 4)
    mask = np.where(np.stack([k <= q, q <= k], 1), 0.0, -1e30).astype(np.float32)
    slopes = np.array([(2.0 ** (-8.0 / H)) ** i for i in range(1, H + 1)], np.float32)
    alibi = (slopes[:, None] * np.arange(T, dtype=np.float32)[None, :]) * np.float32(HD ** 0.5)
    hi = (alibi.view(np.uint32) & np.uint32(0xFFFFF000)).view(np.float32)
    aug = np.stack([hi, alibi - hi, np.ones_like(hi)]).reshape(3, 8, H * T // 8)

    arrays = {
        "xT": x.transpose(0, 2, 1).reshape(nb, KD, P, T).transpose(0, 2, 1, 3),
        "x": x,
        "cT": np.asarray(ctx_768).transpose(0, 2, 1).reshape(nb, KC, PC, NK).transpose(0, 2, 1, 3),
        "wqT": rows(np.asarray(L0_attn_Wq).T), "wkT": rows(np.asarray(L0_attn_Wk).T), "wvT": rows(np.asarray(L0_attn_Wv).T),
        "woS": rows(wo.reshape(-1, D)),
        "xwq": rows(L0_xattn_Wq), "xwk": rows(L0_xattn_Wk, PC), "xwv": rows(L0_xattn_Wv, PC),
        "xwo": rows(xwo.reshape(-1, D)), "bo": np.asarray(L0_xattn_bo),
        "fwT": rows(np.asarray(L0_ffn_weight).T), "fa1": rows(L0_ffn_aux_weight1), "fa2": rows(L0_ffn_aux_weight2),
        "fb": np.asarray(L0_ffn_bias),
        "ident_in": np.concatenate([np.eye(P, dtype=np.float32), in_even, 1 - in_even], 1), "mask_in": mask, "alibi_in": aug,
    }
    nc = bacc.Bacc("TRN2", target_bir_lowering=False, num_devices=1)
    feeds, args = {}, []
    for name, a in arrays.items():
        feeds[f"in_{name}"] = np.ascontiguousarray(a)
        args.append(nc.dram_tensor(f"in_{name}", a.shape, mybir.dt.from_np(a.dtype), kind="ExternalInput").ap())
    out = nc.dram_tensor("out", x.shape, F32, kind="ExternalOutput").ap()
    build_layer(nc, *args, out)
    return run_bass_kernel_spmd(nc, [feeds], core_ids=[0]).results[0]["out"]
```
